# Optimizing a Trainium2 kernel written in Bass

```python
import numpy as np
import jax
import jax.numpy as jnp

def _softmax(x, axis=-1):
    return jax.nn.softmax(x, axis=axis)

def _gelu(x):
    return jax.nn.gelu(x, approximate=True)

def _silu(x):
    return jax.nn.silu(x)

def _sigmoid(x):
    return jax.nn.sigmoid(x)

def _layernorm(x, axis=-1, eps=1e-05):
    m = jnp.mean(x, axis=axis, keepdims=True)
    v = jnp.var(x, axis=axis, keepdims=True)
    return (x - m) / jnp.sqrt(v + eps)

def _scatter_add(tgt, idx, src, axis=0):
    return tgt.at[idx].add(src)

def _segment_sum(src, seg, n):
    return jax.ops.segment_sum(src, seg, n)
kernel_name = 'mk_decoder_postln_d1_seqx_r8_6d6fa4'

def setup_inputs(seed: int=0):
    np.random.seed(seed)
    _w = jnp.asarray

    def _rec_inputs():
        import jax
        import jax.numpy as jnp
        _rk = jax.random.key(seed)
        x = -0.0002928 + 1 * jax.random.normal(jax.random.fold_in(_rk, 1), (32, 128, 128), jnp.float32)
        _lenS = 128 - jax.random.randint(jax.random.fold_in(_rk, 7), (32,), 0, max(1, 128 // 4) + 1, jnp.int32)
        _lenS2 = 128 - jax.random.randint(jax.random.fold_in(_rk, 8), (32,), 0, max(1, 128 // 4) + 1, jnp.int32)
        _ctx_1024P = jax.random.normal(jax.random.fold_in(_rk, 11), (32, 16, 128), jnp.float32)
        _ctx_1024c = jax.random.dirichlet(jax.random.fold_in(_rk, 511), 0.3 * jnp.ones((16,), jnp.float32), (32, 128))
        _ctx_1024t = jnp.einsum('bsk,bkd->bsd', _ctx_1024c, _ctx_1024P)
        _ctx_1024t = _ctx_1024t * jax.lax.rsqrt(jnp.mean(jnp.square(_ctx_1024t)) + 1e-12) * 0.953939
        ctx_1024 = -1.39393e-06 + 0.999914 * (_ctx_1024t + 0.3 * jax.random.normal(jax.random.fold_in(_rk, 611), (32, 128, 128), jnp.float32))
        return (x, ctx_1024)
    x, ctx_1024 = _rec_inputs()

    def _L0_attn_setup():
        import jax, jax.numpy as jnp
        import numpy as np
        EMBED_DIM = 128
        NUM_HEADS = 16
        HEAD_DIM = EMBED_DIM // NUM_HEADS
        FEATURE_EPS = 1e-06
        DEN_EPS = 1e-06
        key = jax.random.key(seed)
        k_x, k_qw, k_qb, k_ow, k_ob = jax.random.split(key, 5)
        b, l = (2, 256)
        x = jax.random.normal(k_x, (b, l, EMBED_DIM), dtype=jnp.float32)
        s = 1.0 / np.sqrt(EMBED_DIM)
        qkv_w = jax.random.uniform(k_qw, (3 * EMBED_DIM, EMBED_DIM), minval=-s, maxval=s, dtype=jnp.float32)
        qkv_b = jax.random.uniform(k_qb, (3 * EMBED_DIM,), minval=-s, maxval=s, dtype=jnp.float32)
        out_w = jax.random.uniform(k_ow, (EMBED_DIM, EMBED_DIM), minval=-s, maxval=s, dtype=jnp.float32)
        out_b = jax.random.uniform(k_ob, (EMBED_DIM,), minval=-s, maxval=s, dtype=jnp.float32)
        return {'x': x, 'qkv_w': qkv_w, 'qkv_b': qkv_b, 'out_w': out_w, 'out_b': out_b}
    _L0_attn_all = _L0_attn_setup()
    _L0_attn_in = {k: v for k, v in _L0_attn_all.items() if k in ('qkv_w', 'qkv_b', 'out_w', 'out_b')}
    del _L0_attn_all

    def _L0_xattn_setup():
        import jax, jax.numpy as jnp
        import numpy as np
        B, T, N_EMBD, N_HEAD = (2, 256, 128, 16)
        HEAD = N_EMBD // N_HEAD
        WINDOW = 64
        key = jax.random.key(seed)
        kq, kk, kv, kw = jax.random.split(key, 4)
        q = jax.random.normal(kq, (B, T, N_EMBD), dtype=jnp.float32)
        k = jax.random.normal(kk, (B, T, N_EMBD), dtype=jnp.float32)
        v = jax.random.normal(kv, (B, T, N_EMBD), dtype=jnp.float32)
        W_proj = jax.random.normal(kw, (N_EMBD, N_EMBD), dtype=jnp.float32) * (1.0 / np.sqrt(N_EMBD))
        b_proj = jnp.zeros((N_EMBD,), dtype=jnp.float32)
        return {'q': q, 'k': k, 'v': v, 'W_proj': W_proj, 'b_proj': b_proj}
    _L0_xattn_all = _L0_xattn_setup()
    _L0_xattn_in = {k: v for k, v in _L0_xattn_all.items() if k in ('W_proj', 'b_proj')}
    del _L0_xattn_all

    def _L0_ffn_setup():
        import jax, jax.numpy as jnp
        import numpy as np
        CAPACITY_FACTOR = 1.25
        key = jax.random.key(seed)
        k1, k2, k3, k4 = jax.random.split(key, 4)
        B, T, D, F, E = (4, 512, 128, 512, 8)
        s = 0.02
        return {'x': jax.random.normal(k1, (B, T, D), dtype=jnp.float32), 'wg': jax.random.normal(k2, (D, E), dtype=jnp.float32) * s, 'W1': jax.random.normal(k3, (E, D, F), dtype=jnp.float32) * s, 'b1': jnp.zeros((E, F), dtype=jnp.float32), 'W2': jax.random.normal(k4, (E, F, D), dtype=jnp.float32) * s, 'b2': jnp.zeros((E, D), dtype=jnp.float32)}
    _L0_ffn_all = _L0_ffn_setup()
    _L0_ffn_in = {k: v for k, v in _L0_ffn_all.items() if k in ('wg', 'W1', 'b1', 'W2', 'b2')}
    del _L0_ffn_all
    return {'x': x, 'ctx_1024': ctx_1024, 'L0_attn_qkv_w': _L0_attn_in['qkv_w'], 'L0_attn_qkv_b': _L0_attn_in['qkv_b'], 'L0_attn_out_w': _L0_attn_in['out_w'], 'L0_attn_out_b': _L0_attn_in['out_b'], 'L0_xattn_W_proj': _L0_xattn_in['W_proj'], 'L0_xattn_b_proj': _L0_xattn_in['b_proj'], 'L0_ffn_wg': _L0_ffn_in['wg'], 'L0_ffn_W1': _L0_ffn_in['W1'], 'L0_ffn_b1': _L0_ffn_in['b1'], 'L0_ffn_W2': _L0_ffn_in['W2'], 'L0_ffn_b2': _L0_ffn_in['b2']}

def reference(x, ctx_1024, L0_attn_qkv_w, L0_attn_qkv_b, L0_attn_out_w, L0_attn_out_b, L0_xattn_W_proj, L0_xattn_b_proj, L0_ffn_wg, L0_ffn_W1, L0_ffn_b1, L0_ffn_W2, L0_ffn_b2):
    import jax
    import jax.numpy as jnp

    def _L0_attn_ref(x, qkv_w, qkv_b, out_w, out_b):
        import jax, jax.numpy as jnp
        import numpy as np
        EMBED_DIM = 128
        NUM_HEADS = 16
        HEAD_DIM = EMBED_DIM // NUM_HEADS
        FEATURE_EPS = 1e-06
        DEN_EPS = 1e-06
        b, l, e = x.shape
        qkv = (x @ qkv_w.T + qkv_b).reshape(b, l, 3, NUM_HEADS, HEAD_DIM)
        qkv = jnp.transpose(qkv, (2, 0, 3, 1, 4))
        q, k, v = (qkv[0], qkv[1], qkv[2])
        q = jax.nn.relu(q) + FEATURE_EPS
        k = jax.nn.relu(k) + FEATURE_EPS
        kv = jnp.cumsum(jnp.einsum('bhld,bhle->bhlde', k, v), axis=2)
        k_cum = jnp.cumsum(k, axis=2)
        num = jnp.einsum('bhld,bhlde->bhle', q, kv)
        den = jnp.maximum(jnp.einsum('bhld,bhld->bhl', q, k_cum)[..., None], DEN_EPS)
        out = num / den
        out = jnp.transpose(out, (0, 2, 1, 3)).reshape(b, l, e)
        return out @ out_w.T + out_b

    def _L0_xattn_ref(q, k, v, W_proj, b_proj):
        import jax, jax.numpy as jnp
        import numpy as np
        B, T, N_EMBD, N_HEAD = (2, 256, 128, 16)
        HEAD = N_EMBD // N_HEAD
        WINDOW = 64
        Bsz, Tlen, _ = q.shape
        qh = q.reshape(Bsz, Tlen, N_HEAD, HEAD).transpose(0, 2, 1, 3)
        kh = k.reshape(Bsz, Tlen, N_HEAD, HEAD).transpose(0, 2, 1, 3)
        vh = v.reshape(Bsz, Tlen, N_HEAD, HEAD).transpose(0, 2, 1, 3)
        scale = 1.0 / np.sqrt(HEAD)
        scores = jnp.einsum('bhqd,bhkd->bhqk', qh, kh) * scale
        idx = jnp.arange(Tlen)
        dist = jnp.abs(idx[None, :] - idx[:, None])
        scores = jnp.where(dist[None, None] > WINDOW, -jnp.inf, scores)
        attn = jax.nn.softmax(scores, axis=-1)
        y = jnp.einsum('bhqk,bhkd->bhqd', attn, vh)
        y = y.transpose(0, 2, 1, 3).reshape(Bsz, Tlen, N_EMBD)
        return y @ W_proj.T + b_proj

    def _L0_ffn_ref(x, wg, W1, b1, W2, b2):
        import jax, jax.numpy as jnp
        import numpy as np
        CAPACITY_FACTOR = 1.25
        B, T, D = x.shape
        E = wg.shape[1]
        N = B * T
        capacity = int(N / E * CAPACITY_FACTOR) + 1
        xf = x.reshape(N, D)
        logits = xf @ wg
        scores = jax.nn.softmax(logits, axis=-1)
        top1 = jnp.argmax(scores, axis=-1)
        combine_w = jnp.take_along_axis(scores, top1[:, None], axis=1)[:, 0]
        oh = jax.nn.one_hot(top1, E, dtype=jnp.int32)
        rank = jnp.take_along_axis(jnp.cumsum(oh, axis=0), top1[:, None], axis=1)[:, 0] - 1
        valid = rank < capacity
        trash = E * capacity
        slot = jnp.where(valid, top1 * capacity + rank, trash)
        buf = jnp.zeros((E * capacity + 1, D), dtype=x.dtype).at[slot].set(xf)
        eb = buf[:E * capacity].reshape(E, capacity, D)
        h = jax.nn.gelu(jnp.einsum('ecd,edf->ecf', eb, W1) + b1[:, None, :], approximate=False)
        y = jnp.einsum('ecf,efd->ecd', h, W2) + b2[:, None, :]
        yf = y.reshape(E * capacity, D)
        gathered = yf[jnp.minimum(slot, E * capacity - 1)]
        out_flat = jnp.where(valid[:, None], gathered, 0.0) * combine_w[:, None]
        return out_flat.reshape(B, T, D)
    x = _layernorm(x + _L0_attn_ref(x, L0_attn_qkv_w, L0_attn_qkv_b, L0_attn_out_w, L0_attn_out_b), axis=-1)
    x = _layernorm(x + _L0_xattn_ref(x, ctx_1024, ctx_1024, L0_xattn_W_proj, L0_xattn_b_proj), axis=-1)
    x = _layernorm(x + _L0_ffn_ref(x, L0_ffn_wg, L0_ffn_W1, L0_ffn_b1, L0_ffn_W2, L0_ffn_b2), axis=-1)
    return x

_drawn_inputs = setup_inputs


def setup_inputs(seed=0):
    import zlib

    import numpy as np

    out = dict(_drawn_inputs(seed))
    spreads = {'L0_xattn_b_proj': (0.0, 0.1), 'L0_ffn_b1': (0.0, 0.8), 'L0_ffn_b2': (0.0, 0.477)}
    factors = {'L0_ffn_wg': 3.092, 'L0_ffn_W1': 6.204, 'L0_ffn_W2': 5.634}
    for name, (base, spread) in spreads.items():
        noise = np.random.default_rng([zlib.crc32(name.encode()), seed]).standard_normal(out[name].shape)
        drawn = base * np.exp(spread * noise) if base else spread * noise
        out[name] = jnp.asarray(drawn.astype(out[name].dtype))
    for name, factor in factors.items():
        out[name] = (out[name] * factor).astype(out[name].dtype)
    return out
```

```python
from contextlib import ExitStack

import concourse.bass as bass
from concourse import mybir

F32 = mybir.dt.float32
F32R = mybir.dt.float32r
BF16 = mybir.dt.bfloat16
U32 = mybir.dt.uint32
ALU = mybir.AluOpType
ACT = mybir.ActivationFunctionType
AX_X = mybir.AxisListType.X

P = 128
UNROLL = 4
FEATURE_EPS = 1e-6
DEN_EPS = 1e-6
LN_EPS = 1e-5
MASKED = -1e30
WINDOW = 64
HALVES = 4

ACT_JOBS = ([("s1", u, 1) for u in range(4)] + [("kx2", 0, 2), ("qx2", 0, 2)]
            + [("s2t", u, 3) for u in range(4)] + [("qx", 0, 0), ("kx", 0, 0), ("qm", 0, 2)])
DVE_JOBS = [("xT", 0, 0), ("x2T", 0, 4), ("qkv", 0, 0), ("lg", 0, 4), ("y1", 0, 1), ("y2", 0, 3),
            ("rk", 0, 4), ("y1T", 0, 1), ("y2T", 0, 3), ("o1", 0, 1), ("o2", 0, 3)]


class Step:

    def __init__(self, n, i=None, batches=32):
        self.n, self.i, self.batches = n, i, batches

    def has(self, lag):
        return 0 <= self.n - lag < self.batches

    def lin(self, value, per_step):
        return value if self.i is None else self.i * (per_step * UNROLL) + value

    def batch(self, lag):
        return self.lin(self.n - lag, 1)

    def slot(self, lag, ring):
        return (self.n - lag) % ring

    def upto(self, lag, per_batch=1, back=0, extra=0):
        if self.n - lag - back < 0:
            return None
        return self.lin((self.n - lag - back + 1) * per_batch + extra, per_batch)

    def job(self, jobs, name, u, lag, back=0):
        at = [k for k, j in enumerate(jobs) if j[0] == name and j[1] == u][0]
        step = self.n - lag - back + jobs[at][2]
        if self.n - lag - back < 0:
            return None
        return self.lin(step * len(jobs) + at + 1, len(jobs))


class Seq:

    def __init__(self, eng, sem, per_step, behind):
        self.eng, self.sem, self.n, self.per_step, self.i, self.behind = eng, sem, 0, per_step, None, behind

    def mark(self, ins):
        self.n += 1
        ins.then_inc(self.sem, 1)
        return self.n

    def wait(self, alone=False):
        n = self.n if self.i is None else self.i * (self.per_step * UNROLL) + self.n
        wait(self.eng, self.sem, n, self.behind if alone else None)


def wait(eng, sem, value, behind=None):
    if value is None or (isinstance(value, int) and value <= 0):
        return
    eng.wait_ge(sem, value)
    if behind is not None and not isinstance(value, int):
        eng.sem_inc(behind, 1)


def decoder(nc, x, ctx_in, qkv_w, qkv_b, out_w, out_b, proj_w, proj_b, wg, W1, b1, W2, b2, out):
    B, T, D = x.shape
    E, _, F = W1.shape
    HD = 8
    H = D // HD
    G = P // (HALVES * HD)
    NA = H // G
    N = B * T
    CAP = int(N / E * 1.25) + 1
    ET = -(-CAP // P)
    ER = -(-CAP // ET)
    CAPP = ER * ET
    TRASH = E * CAPP
    FC = F // P
    HALF = CAPP // 2
    LAST = 4
    LOOP = (2 * UNROLL, B)
    SCALE = float(HD) ** -0.5
    BIG = 1e6
    assert T == P and D == P and CAPP % 2 == 0 and B % UNROLL == 0

    buf = nc.dram_tensor("expert_in", [TRASH, D], F32, kind="Internal").ap()
    ybuf = nc.dram_tensor("expert_out", [TRASH + 1, D], F32, kind="Internal").ap()

    ctx = ExitStack()
    with ctx:
        def sb(name, shape, dt=F32):
            return ctx.enter_context(nc.sbuf_tensor(name, shape, dt))

        def ring(name, n, shape, dt=F32):
            return [sb(f"{name}{k}", shape, dt) for k in range(n)]

        def sem(name):
            return ctx.enter_context(nc.semaphore(name))

        act_bank = [ctx.enter_context(nc.psum_tensor(f"act_bank{k}", [P, 512], F32)) for k in range(4)]
        max_bank = [ctx.enter_context(nc.psum_tensor(f"max_bank{k}", [P, 512], F32)) for k in range(2)]
        dve_bank = [ctx.enter_context(nc.psum_tensor(f"dve_bank{k}", [P, 512], F32)) for k in range(2)]

        ident = sb("ident", [P, P])
        identb = sb("identb", [P, P], BF16)
        upto_t = sb("upto_t", [P, P], BF16)
        onesb = sb("onesb", [P, P], BF16)
        window = sb("window", [P, NA, P], BF16)
        zeros = sb("zeros", [P, TRASH // 4])
        minus_half = sb("minus_half", [P, 4])
        rank_w = sb("rank_w", [P, E])

        w_rows = sb("w_rows", [P, 5, D])
        wqkvT = sb("wqkvT", [P, 3 * D])
        woT = sb("woT", [P, D])
        wpT = sb("wpT", [P, D])
        wg_sb = sb("wg_sb", [P, E])
        b1_rows = sb("b1_rows", [E * FC, P])
        b1T = sb("b1T", [P, E * FC])
        qkvb = sb("qkvb", [P, 3 * D])
        outb = sb("outb", [P, D])
        projb = sb("projb", [P, D])
        b2b = sb("b2b", [P, E, D])

        X = ring("X", 4, [P, D])
        C = ring("C", 4, [P, D])
        xb = ring("xb", 2, [P, D])
        xT = ring("xT", 2, [P, P])
        qk = ring("qk", 2, [P, 2 * D])
        qkz = sb("qkz", [P, 2 * D])
        V1 = ring("V1", 2, [P, H, HD + 1])
        QX = ring("QX", 2, [P, H, HALVES, HD], F32R)
        KX = ring("KX", 2, [P, H, HALVES, HD], F32R)
        QT = ring("QT", 2, [P, NA, P], F32R)
        KT = ring("KT", 2, [P, NA, P], F32R)
        A1 = ring("A1", 2, [P, G, NA, P])
        den1 = sb("den1", [P, H])
        rden1 = sb("rden1", [P, H])
        y1 = ring("y1", 2, [P, H, HD])
        y1T = ring("y1T", 2, [P, P])
        r1 = sb("r1", [P, D])
        st1 = sb("st1", [P, 6])
        mv1 = sb("mv1", [P, 2])
        ve1 = sb("ve1", [P, 1])
        rs1 = sb("rs1", [P, 1])
        x1 = ring("x1", 2, [P, D])
        x1b = ring("x1b", 4, [P, D])
        QX2 = ring("QX2", 2, [P, H, HALVES, HD], F32R)
        KX2 = ring("KX2", 2, [P, H, HALVES, HD], F32R)
        V2 = ring("V2", 4, [P, H, HD + 1])
        QT2 = ring("QT2", 2, [P, NA, P], F32R)
        QM2 = ring("QM2", 2, [P, NA, P], F32R)
        KT2 = ring("KT2", 2, [P, NA, P], F32R)
        mx = ring("mx", 2, [P, NA, G])
        P2 = ring("P2", 2, [P, G, NA, P])
        rden2 = sb("rden2", [P, H])
        y2 = ring("y2", 2, [P, H, HD])
        y2T = ring("y2T", 2, [P, P])
        r2 = sb("r2", [P, D])
        st2 = sb("st2", [P, 6])
        mv2 = sb("mv2", [P, 2])
        ve2 = sb("ve2", [P, 1])
        rs2 = sb("rs2", [P, 1])
        x2 = ring("x2", 4, [P, D])
        x2T = ring("x2T", 2, [P, P])
        x2_all = sb("x2_all", [P, B, D])
        lg = ring("lg", 2, [P, E])
        lmax = sb("lmax", [P, 1])
        nlmax = ring("nlmax", 2, [P, 1])
        lexp = sb("lexp", [P, E])
        esum = ring("esum", 2, [P, 1])
        cand = sb("cand", [P, E])
        top = ring("top", 2, [P, 1])
        oh = ring("oh", 2, [P, E], BF16)
        carry = ring("carry", 2, [P, E])
        rc = sb("rc", [P, E])
        rcoh = sb("rcoh", [P, E])
        rank = sb("rank", [P, 1])
        slot0 = sb("slot0", [P, 1])
        slot1 = sb("slot1", [P, 1])
        over = sb("over", [P, 1])
        slot2 = sb("slot2", [P, 1])
        valid = sb("valid", [P, 1])
        rsum = sb("rsum", [P, 1])
        sidx = ring("sidx", 4, [P, 1], U32)
        gidx_all = sb("gidx_all", [P, B], U32)
        gate_all = sb("gate_all", [P, B])
        w1_sb = ring("w1_sb", 2, [P, F])
        w2_sb = ring("w2_sb", 2, [P, FC, D])
        EB = ring("EB", 2, [ER, ET, D])
        ebT = ring("ebT", 2, [P, ET, ER])
        hT = ring("hT", 2, [P, FC, CAPP])
        yE = ring("yE", 2, [ER, ET, D])
        GR = 4
        gi = ring("gi", 8, [P, 1], U32)
        gy = ring("gy", 2, [P, GR, D])
        r3 = ring("r3", 2, [P, GR, D])
        st3 = sb("st3", [P, GR, 6])
        mv3 = ring("mv3", 2, [P, GR, 2])
        ve3 = ring("ve3", 2, [P, GR])
        rs3 = ring("rs3", 2, [P, GR])
        ot = ring("ot", 2, [P, GR, D])

        weights_in = sem("weights_in")
        zeros_out = sem("zeros_out")
        x_in = [sem(f"x_in{k}") for k in range(4)]
        consts = sem("consts")
        setup_full = sem("setup_full")
        setup_done = sem("setup_done")
        act_full = sem("act_full")
        act_done = sem("act_done")
        max_full = sem("max_full")
        max_done = sem("max_done")
        dve_full = sem("dve_full")
        dve_done = sem("dve_done")
        causal = sem("causal")
        xb_ready = sem("xb_ready")
        qk_ready = sem("qk_ready")
        qkx_ready = sem("qkx_ready")
        kv2_ready = sem("kv2_ready")
        qx2_ready = sem("qx2_ready")
        qm_ready = sem("qm_ready")
        var1_ready = sem("var1_ready")
        rstd1_ready = sem("rstd1_ready")
        x1_ready = sem("x1_ready")
        var2_ready = sem("var2_ready")
        rstd2_ready = sem("rstd2_ready")
        x2_ready = sem("x2_ready")
        x2_kept = sem("x2_kept")
        logits_ready = sem("logits_ready")
        esum_ready = sem("esum_ready")
        oh_ready = sem("oh_ready")
        slot_ready = sem("slot_ready")
        scattered = [sem(f"scattered{k}") for k in range(4)]
        dve_own = sem("dve_own")
        pool_own = sem("pool_own")
        w_in = [sem(f"w_in{k}") for k in range(2)]
        eb_in = [sem(f"eb_in{k}") for k in range(2)]
        t_full = sem("t_full")
        t_done = sem("t_done")
        h_full = sem("h_full")
        h_done = sem("h_done")
        y_full = sem("y_full")
        y_done = sem("y_done")
        ye_out = [sem(f"ye_out{k}") for k in range(2)]
        passed = sem("passed")
        gi_ready = sem("gi_ready")
        gathered = [sem(f"gathered{k}") for k in range(2)]
        var3_ready = sem("var3_ready")
        rstd3_ready = sem("rstd3_ready")
        ot_ready = sem("ot_ready")
        comb_own = sem("comb_own")
        out_done = [sem(f"out_done{k}") for k in range(2)]

        CONSTS = 14
        COMB = 3 * GR
        NW = 14
        block = ctx.enter_context(nc.Block())

        def act_slot(s, name, u, lag):
            at = [k for k, j in enumerate(ACT_JOBS) if j[0] == name and j[1] == u][0]
            return act_bank[(s.n * len(ACT_JOBS) + at) % 4]

        def dve_slot(s, name):
            at = [k for k, j in enumerate(DVE_JOBS) if j[0] == name][0]
            return dve_bank[(s.n * len(DVE_JOBS) + at) % 2]

        def lag_of(jobs, name):
            return [j[2] for j in jobs if j[0] == name][0]

        def run(eng, step):
            for n in range(LOOP[0]):
                step(Step(n))
            with eng.Fori(0, (LOOP[1] - LOOP[0]) // UNROLL) as i:
                for k in range(UNROLL):
                    step(Step(LOOP[0] + k, i))
            for n in range(LOOP[1], B + LAST):
                step(Step(n))

        def run_own(eng, own, step):
            for n in range(LOOP[0]):
                step(Step(n))
            start = own.n
            with eng.Fori(0, (LOOP[1] - LOOP[0]) // UNROLL) as i:
                own.i = i
                for k in range(UNROLL):
                    step(Step(LOOP[0] + k, i))
            assert own.n - start == own.per_step * UNROLL, (own.n - start, own.per_step)
            own.i = None
            own.n = start + own.per_step * (LOOP[1] - LOOP[0])
            for n in range(LOOP[1], B + LAST):
                step(Step(n))

        @block.sync
        def _(sp):
            def load_batch(b, k):
                sp.dma_start(X[k][:], x[b]).then_inc(x_in[k], 16)
                sp.dma_start(C[k][:], ctx_in[b]).then_inc(x_in[k], 16)

            for count in (t_done, h_full, h_done, y_full, y_done, gi_ready, var3_ready):
                sp.sem_inc(count, 1)
            for k in range(2):
                sp.sem_inc(ye_out[k], 16)
                sp.sem_inc(out_done[k], 16)
            sp.dma_start(w_rows[:, 0:3, :], qkv_w.rearrange("(k p) d -> p k d", p=P)).then_inc(weights_in, 16)
            load_batch(0, 0)
            sp.dma_start(w_rows[:, 3, :], out_w).then_inc(weights_in, 16)
            sp.dma_start(w_rows[:, 4, :], proj_w).then_inc(weights_in, 16)
            sp.dma_start(wg_sb[:], wg).then_inc(weights_in, 16)
            sp.dma_start(b1_rows[:], b1.rearrange("e (k p) -> (e k) p", p=P)).then_inc(weights_in, 16)
            sp.dma_start(qkvb[:], qkv_b.unsqueeze(0).broadcast_to([P, 3 * D])).then_inc(weights_in, 16)
            sp.dma_start(outb[:], out_b.unsqueeze(0).broadcast_to([P, D])).then_inc(weights_in, 16)
            sp.dma_start(projb[:], proj_b.unsqueeze(0).broadcast_to([P, D])).then_inc(weights_in, 16)
            sp.dma_start(b2b[:], b2.unsqueeze(0).broadcast_to([P, E, D])).then_inc(weights_in, 16)
            for k in range(1, 4):
                load_batch(k, k)
            sp.wait_ge(consts, 1)
            zview = buf.rearrange("n d -> (n d)").rearrange("(p f) -> p f", p=P)
            quarter = TRASH // 4
            for k in range(4):
                sp.dma_start(zview[:, k * quarter:(k + 1) * quarter], zeros[:]).then_inc(zeros_out, 16)
            sp.dma_start(ybuf[TRASH:TRASH + 1, :], zeros[0:1, 0:D]).then_inc(zeros_out, 16)
            with sp.Fori(0, (B - 4) // 4) as i:
                for k in range(4):
                    s = Step(4 + k, i)
                    wait(sp, dve_full, s.job(DVE_JOBS, "xT", 0, 0, 4), passed)
                    wait(sp, xb_ready, s.upto(0, 1, 4), passed)
                    wait(sp, kv2_ready, s.upto(0, 1, 4), passed)
                    sp.dma_start(X[k][:], x[bass.ds(s.batch(0), 1)].rearrange("o t d -> (o t) d")).then_inc(x_in[k], 16)
                    sp.dma_start(C[k][:], ctx_in[bass.ds(s.batch(0), 1)].rearrange("o t d -> (o t) d")).then_inc(x_in[k], 16)

            def expert_rows(e, k, i):
                src = buf[e * CAPP:(e + 1) * CAPP, :] if i is None else buf[bass.ds(i * (2 * CAPP) + k * CAPP, CAPP), :]
                sp.dma_start(EB[k][:], src.rearrange("(c p) d -> p c d", p=ER)).then_inc(eb_in[k], 16)

            def expert_weights(e, k, i):
                w1 = W1[e] if i is None else W1[bass.ds(i * 2 + k, 1)].rearrange("o d f -> (o d) f")
                w2 = W2[e:e + 1] if i is None else W2[bass.ds(i * 2 + k, 1)]
                sp.dma_start(w1_sb[k][:], w1).then_inc(w_in[k], 16)
                sp.dma_start(w2_sb[k][:], w2.rearrange("o (c p) d -> p (o c) d", p=P)).then_inc(w_in[k], 16)

            expert_weights(0, 0, None)
            expert_weights(1, 1, None)
            for k in range(4):
                sp.wait_ge(scattered[k], 16 * (B // 4))
            expert_rows(0, 0, None)
            expert_rows(1, 1, None)

            def store_y(k, i):
                wait(sp, y_done, i * (2 * ET) + (k + 1) * ET + 1, passed)
                dst = ybuf[bass.ds(i * (2 * CAPP) + k * CAPP, CAPP), :]
                sp.dma_start(dst.rearrange("(c p) d -> p c d", p=ER), yE[k][:]).then_inc(ye_out[k], 16)

            with sp.Fori(0, E // 2 - 1) as i:
                for k in range(2):
                    store_y(k, i)
                    wait(sp, y_full, i * (2 * ET) + (k + 1) * ET + 1, passed)
                    w1 = W1[bass.ds(i * 2 + (k + 2), 1)].rearrange("o d f -> (o d) f")
                    w2 = W2[bass.ds(i * 2 + (k + 2), 1)]
                    sp.dma_start(w1_sb[k][:], w1).then_inc(w_in[k], 16)
                    sp.dma_start(w2_sb[k][:], w2.rearrange("o (c p) d -> p (o c) d", p=P)).then_inc(w_in[k], 16)
                    src = buf[bass.ds(i * (2 * CAPP) + (k + 2) * CAPP, CAPP), :]
                    sp.dma_start(EB[k][:], src.rearrange("(c p) d -> p c d", p=ER)).then_inc(eb_in[k], 16)
            for k in range(2):
                e = E - 2 + k
                sp.wait_ge(y_done, (e + 1) * ET + 1)
                sp.dma_start(ybuf[e * CAPP:(e + 1) * CAPP, :].rearrange("(c p) d -> p c d", p=ER),
                             yE[k][:]).then_inc(ye_out[k], 16)

            with sp.Fori(0, B // GR // 2) as i:
                for k in range(2):
                    wait(sp, ot_ready, i * (2 * GR) + (k + 1) * GR, passed)
                    dst = out[bass.ds(i * (2 * GR) + k * GR, GR)]
                    sp.dma_start(dst.rearrange("b t d -> t b d"), ot[k][:]).then_inc(out_done[k], 16)
            for k in range(2):
                sp.wait_ge(out_done[k], 16 * (B // GR // 2) + 16)

        @block.gpsimd
        def _(pool):
            g = nc.gpsimd
            g.memset(zeros[:], 0.0).then_inc(consts, 1)
            g.memset(ident[:], 0.0).then_inc(consts, 1)
            g.memset(identb[:], 0.0).then_inc(consts, 1)
            g.memset(upto_t[:], 1.0).then_inc(consts, 1)
            g.memset(onesb[:], 1.0).then_inc(consts, 1)
            g.memset(window[:], 0.0).then_inc(consts, 1)
            g.memset(minus_half[:], -0.5).then_inc(consts, 1)
            pool.wait_ge(consts, 7)
            diag = dict(pattern=[[-1, P]], channel_multiplier=1, base=0)
            g.affine_select(out=ident[:], in_=ident[:], compare_op=ALU.not_equal, fill=1.0, **diag).then_inc(consts, 1)
            g.affine_select(out=identb[:], in_=identb[:], compare_op=ALU.not_equal, fill=1.0, **diag).then_inc(consts, 1)
            g.affine_select(out=upto_t[:], in_=upto_t[:], compare_op=ALU.is_ge, fill=0.0, base=0,
                            pattern=[[1, P]], channel_multiplier=-1).then_inc(consts, 1)
            g.affine_select(out=window[:], in_=window[:], compare_op=ALU.is_ge, fill=MASKED, base=WINDOW,
                            pattern=[[0, NA], [1, P]], channel_multiplier=-1).then_inc(consts, 1)
            pool.wait_ge(consts, 11)
            g.affine_select(out=window[:], in_=window[:], compare_op=ALU.is_ge, fill=MASKED, base=WINDOW,
                            pattern=[[0, NA], [-1, P]], channel_multiplier=1).then_inc(consts, 1)
            for e in range(E):
                last = g.memset(rank_w[:, e:e + 1], float(E - e))
            last.then_inc(consts, 1)
            for k in range(2):
                g.memset(V1[k][:], 1.0)
                g.memset(QX2[k][:].bitcast(F32), 0.0)
                g.memset(KX2[k][:].bitcast(F32), -1.0)
                g.memset(carry[k][:], 0.0)
            for k in range(4):
                last = g.memset(V2[k][:], 1.0)
            last.then_inc(consts, 1)
            pool.wait_ge(consts, CONSTS)
            pool.wait_ge(weights_in, 16 * 9)
            own = Seq(pool, pool_own, 5, passed)

            def heads(ap):
                return ap.rearrange("p (h d) -> p h d", d=HD)

            def twice(ap):
                return ap.unsqueeze(2).broadcast_to([P, H, 2, HD])

            def step(s):
                if s.has(1):
                    for u in range(G):
                        wait(pool, act_done, s.job(ACT_JOBS, "s1", u, 1), passed)
                        a = A1[s.slot(1, 2)][:, u]
                        g.affine_select(out=a, in_=a, compare_op=ALU.is_ge, fill=0.0, base=0,
                                        pattern=[[0, NA], [1, P]], channel_multiplier=-1).then_inc(causal, 1)
                if s.has(0):
                    k = s.slot(0, 4)
                    wait(pool, x_in[k], 32 * (s.n // 4 + 1) if s.i is None else s.i * 32 + 32 * (s.n // 4 + 1), passed)
                    wait(pool, var1_ready, s.upto(0, 1, 2), passed)
                    g.tensor_tensor(xb[s.slot(0, 2)][:], X[k][:], outb[:], ALU.add).then_inc(xb_ready, 1)
                if s.has(1):
                    kx, v2, c = KX2[s.slot(1, 2)], V2[s.slot(1, 4)], heads(C[s.slot(1, 4)][:])
                    wait(pool, act_full, s.job(ACT_JOBS, "kx2", 0, 1, 2), passed)
                    own.mark(g.tensor_copy(kx[:, :, 0:3:2, :], twice(c)))
                    wait(pool, dve_full, s.job(DVE_JOBS, "y2", 0, 1, 4), passed)
                    g.tensor_copy(v2[:, :, 0:HD], c)
                    own.wait()
                    g.tensor_tensor(kx[:, :, 1, :], c, kx[:, :, 0, :].bitcast(F32), ALU.subtract).then_inc(kv2_ready, 1)
                if s.has(0):
                    q, kk = heads(qk[s.slot(0, 2)][:, 0:D]), heads(qk[s.slot(0, 2)][:, D:2 * D])
                    qx, kx = QX[s.slot(0, 2)], KX[s.slot(0, 2)]
                    wait(pool, qk_ready, s.upto(0), passed)
                    wait(pool, act_full, s.job(ACT_JOBS, "kx", 0, 0, 2), passed)
                    own.mark(g.tensor_copy(qx[:, :, 0:2, :], twice(q)))
                    own.mark(g.tensor_copy(kx[:, :, 0:4:2, :], twice(kk)))
                    own.wait()
                    g.tensor_tensor(qx[:, :, 2:4, :], twice(q), qx[:, :, 0:2, :].bitcast(F32), ALU.subtract)
                    g.tensor_tensor(kx[:, :, 1:4:2, :], twice(kk), kx[:, :, 0:4:2, :].bitcast(F32),
                                    ALU.subtract).then_inc(qkx_ready, 1)
                if s.has(2):
                    qx = QX2[s.slot(2, 2)][:, :, 3, :]
                    m = mx[s.slot(2, 2)][:].rearrange("p a j -> p (a j)").unsqueeze(2)
                    wait(pool, max_done, s.upto(2, G), passed)
                    wait(pool, act_full, s.job(ACT_JOBS, "qx2", 0, 2), passed)
                    own.mark(g.tensor_copy(qx[:, :, 0:1], m))
                    own.wait()
                    g.tensor_tensor(qx[:, :, 1:2], m, qx[:, :, 0:1].bitcast(F32), ALU.subtract).then_inc(qm_ready, 1)
                if s.has(1):
                    wait(pool, var1_ready, s.upto(1), passed)
                    g.tensor_tensor(rs1[:], ve1[:], minus_half[:, 0:1], ALU.pow).then_inc(rstd1_ready, 1)
                if s.has(3):
                    wait(pool, var2_ready, s.upto(3), passed)
                    g.tensor_tensor(rs2[:], ve2[:], minus_half[:, 0:1], ALU.pow).then_inc(rstd2_ready, 1)
                if s.has(1):
                    xx, qx = x1[s.slot(1, 2)], QX2[s.slot(1, 2)]
                    wait(pool, x1_ready, s.upto(1), passed)
                    wait(pool, act_full, s.job(ACT_JOBS, "qm", 0, 1, 2), passed)
                    own.mark(g.tensor_copy(qx[:, :, 0:2, :], twice(heads(xx[:]))))
                    wait(pool, var2_ready, s.upto(1, 1, 4), passed)
                    g.tensor_tensor(x1b[s.slot(1, 4)][:], xx[:], projb[:], ALU.add)
                    own.wait()
                    g.tensor_tensor(qx[:, :, 2, :], heads(xx[:]), qx[:, :, 0, :].bitcast(F32),
                                    ALU.subtract).then_inc(qx2_ready, 1)
                if s.has(4):
                    k = s.slot(4, 4)
                    wait(pool, x2_ready, s.upto(4), passed)
                    g.tensor_copy(x2_all[:, bass.ds(s.batch(4), 1), :].rearrange("p o d -> p (o d)"),
                                  x2[k][:]).then_inc(x2_kept, 1)
                    wait(pool, slot_ready, s.upto(4), passed)
                    if s.n == 4:
                        pool.wait_ge(zeros_out, 16 * 5)
                    g.indirect_dma_start(out=buf, out_offset=bass.IndirectOffsetOnAxis(ap=sidx[k][:], axis=0),
                                         in_=x2[k][:], in_offset=None, bounds_check=TRASH - 1,
                                         oob_is_err=False).then_inc(scattered[k], 16)

            run_own(pool, own, step)

            pool.wait_ge(zeros_out, 16 * 5)
            for k in range(2):
                pool.wait_ge(ye_out[k], 16 * (E // 2) + 16)
            pool.wait_ge(slot_ready, B)
            with pool.Fori(0, B // GR // 2) as i:
                for k in range(2):
                    wait(pool, gi_ready, i * (2 * GR) + k * GR + 1, passed)
                    wait(pool, var3_ready, i * 2 + 1, passed)
                    for c in range(GR):
                        g.tensor_copy(gi[k * GR + c][:], gidx_all[:, bass.ds(i * (2 * GR) + (k * GR + c), 1)]).then_inc(gi_ready, 1)
                    wait(pool, gi_ready, i * (2 * GR) + (k + 1) * GR + 1, passed)
                    for c in range(GR):
                        g.indirect_dma_start(out=gy[k][:, c, :], out_offset=None, in_=ybuf,
                                             in_offset=bass.IndirectOffsetOnAxis(ap=gi[k * GR + c][:], axis=0),
                                             bounds_check=TRASH, oob_is_err=False).then_inc(gathered[k], 16)
                    wait(pool, var3_ready, i * 2 + (k + 1) + 1, passed)
                    g.tensor_tensor(rs3[k][:], ve3[k][:], minus_half[:, 0:GR], ALU.pow).then_inc(rstd3_ready, 1)

        @block.tensor
        def _(pe):
            pe.wait_ge(consts, CONSTS)
            pe.wait_ge(weights_in, 16 * 9)
            for k in range(4):
                pe.transpose(max_bank[0][:, k * P:(k + 1) * P], w_rows[:, k, :], ident[:])
            pe.transpose(max_bank[1][:, 0:P], w_rows[:, 4, :], ident[:])
            pe.transpose(max_bank[1][:, P:P + E * FC], b1_rows[:], ident[0:E * FC, 0:E * FC]).then_inc(setup_full, 1)
            pe.wait_ge(setup_done, 1)

            def act_take(s, name, u=0):
                at = [k for k, j in enumerate(ACT_JOBS) if j[0] == name and j[1] == u][0]
                n = s.n * len(ACT_JOBS) + at
                if n >= 4:
                    wait(pe, act_done, s.lin(n - 3, len(ACT_JOBS)))
                return act_bank[n % 4]

            def dve_take(s, name):
                at = [k for k, j in enumerate(DVE_JOBS) if j[0] == name][0]
                n = s.n * len(DVE_JOBS) + at
                if n >= 2:
                    wait(pe, dve_done, s.lin(n - 1, len(DVE_JOBS)))
                return dve_bank[n % 2]

            def transposed(s, name, src, lag, ready, value):
                if not s.has(lag):
                    pe.drain().then_inc(act_full, 1)
                    return
                bank = act_take(s, name)
                wait(pe, ready, value)
                for a in range(NA):
                    mm = pe.transpose(bank[:, a * P:(a + 1) * P],
                                      src[:, a * G:(a + 1) * G].rearrange("p j c d -> p (j c d)").bitcast(F32), ident[:])
                mm.then_inc(act_full, 1)

            def small(s, name, lag):
                if not s.has(lag):
                    pe.drain().then_inc(dve_full, 1)
                    return None
                return dve_take(s, name)

            def weighted(s, name, lag, scores, V):
                bank = small(s, name, lag)
                if bank is None:
                    return
                for u in range(G):
                    if name == "y1":
                        wait(pe, causal, s.upto(lag, G, 0, u + 1 - G))
                    else:
                        wait(pe, act_done, s.job(ACT_JOBS, "s2t", u, lag))
                    for a in range(NA):
                        h = a * G + u
                        mm = pe.matmul(bank[:, h * (HD + 1):(h + 1) * (HD + 1)], scores[:, u, a, :],
                                       V[:, h, :], start=True, stop=True)
                mm.then_inc(dve_full, 1)

            def step(s):
                bank = small(s, "xT", 0)
                if bank is not None:
                    k = s.slot(0, 4)
                    wait(pe, x_in[k], 32 * (s.n // 4 + 1) if s.i is None else s.i * 32 + 32 * (s.n // 4 + 1))
                    pe.transpose(bank[:, 0:P], X[k][:], ident[:]).then_inc(dve_full, 1)
                bank = small(s, "x2T", 4)
                if bank is not None:
                    wait(pe, x2_ready, s.upto(4))
                    pe.transpose(bank[:, 0:P], x2[s.slot(4, 4)][:], ident[:]).then_inc(dve_full, 1)
                for u in range(G):
                    if not s.has(1):
                        pe.drain().then_inc(act_full, 1)
                        continue
                    bank = act_take(s, "s1", u)
                    if u == 0:
                        wait(pe, act_done, s.job(ACT_JOBS, "kx", 0, 1))
                    rows = slice(32 * u, 32 * u + 32)
                    for a in range(NA):
                        mm = pe.matmul(bank[:, a * P:(a + 1) * P], KT[s.slot(1, 2)][rows, a, :],
                                       QT[s.slot(1, 2)][rows, a, :], start=True, stop=True)
                    mm.then_inc(act_full, 1)
                transposed(s, "kx2", KX2[s.slot(2, 2)], 2, kv2_ready, s.upto(2))
                transposed(s, "qx2", QX2[s.slot(2, 2)], 2, qx2_ready, s.upto(2))
                bank = small(s, "qkv", 0)
                if bank is not None:
                    wait(pe, dve_done, s.job(DVE_JOBS, "xT", 0, 0))
                    pe.matmul(bank[:, 0:3 * D], xT[s.slot(0, 2)][:], wqkvT[:], start=True, stop=True).then_inc(dve_full, 1)
                bank = small(s, "lg", 4)
                if bank is not None:
                    wait(pe, dve_done, s.job(DVE_JOBS, "x2T", 0, 4))
                    pe.matmul(bank[:, 0:E], x2T[s.slot(4, 2)][:], wg_sb[:], start=True, stop=True).then_inc(dve_full, 1)
                for u in range(G):
                    if not s.has(3):
                        pe.drain().then_inc(act_full, 1)
                        continue
                    bank = act_take(s, "s2t", u)
                    if u == 0:
                        wait(pe, act_done, s.job(ACT_JOBS, "qm", 0, 3))
                    rows = slice(32 * u, 32 * u + 32)
                    pe.matmul(bank[:], identb[:], window[:].rearrange("p a c -> p (a c)"), start=True, stop=False)
                    for a in range(NA):
                        mm = pe.matmul(bank[:, a * P:(a + 1) * P], KT2[s.slot(3, 2)][rows, a, :],
                                       QM2[s.slot(3, 2)][rows, a, :], start=False, stop=(a == NA - 1))
                    mm.then_inc(act_full, 1)
                if s.has(2):
                    for u in range(G):
                        if s.n > 2 or u >= 2:
                            wait(pe, max_done, s.upto(2, G, 0, u - G - 1))
                        if u == 0:
                            wait(pe, act_done, s.job(ACT_JOBS, "qx2", 0, 2))
                        rows = slice(32 * u, 32 * u + 24)
                        bank = max_bank[u % 2]
                        pe.matmul(bank[:], identb[:], window[:].rearrange("p a c -> p (a c)"), start=True, stop=False)
                        for a in range(NA):
                            mm = pe.matmul(bank[:, a * P:(a + 1) * P], QT2[s.slot(2, 2)][rows, a, :],
                                           KT2[s.slot(2, 2)][rows, a, :], start=False, stop=(a == NA - 1))
                        mm.then_inc(max_full, 1)
                weighted(s, "y1", 1, A1[s.slot(1, 2)], V1[s.slot(1, 2)])
                if s.has(3):
                    wait(pe, kv2_ready, s.upto(3))
                weighted(s, "y2", 3, P2[s.slot(3, 2)], V2[s.slot(3, 4)])
                bank = small(s, "rk", 4)
                if bank is not None:
                    wait(pe, oh_ready, s.upto(4))
                    pe.matmul(bank[:, 0:E], upto_t[:], oh[s.slot(4, 2)][:], start=True, stop=True)
                    pe.matmul(bank[:, E:2 * E], onesb[:], oh[s.slot(4, 2)][:], start=True, stop=True).then_inc(dve_full, 1)
                transposed(s, "qx", QX[s.slot(0, 2)], 0, qkx_ready, s.upto(0))
                transposed(s, "kx", KX[s.slot(0, 2)], 0, qkx_ready, s.upto(0))
                bank = small(s, "y1T", 1)
                if bank is not None:
                    wait(pe, dve_done, s.job(DVE_JOBS, "y1", 0, 1))
                    pe.transpose(bank[:, 0:P], y1[s.slot(1, 2)][:].rearrange("p h d -> p (h d)"), ident[:]).then_inc(dve_full, 1)
                bank = small(s, "y2T", 3)
                if bank is not None:
                    wait(pe, dve_done, s.job(DVE_JOBS, "y2", 0, 3))
                    pe.transpose(bank[:, 0:P], y2[s.slot(3, 2)][:].rearrange("p h d -> p (h d)"), ident[:]).then_inc(dve_full, 1)
                transposed(s, "qm", QX2[s.slot(2, 2)], 2, qm_ready, s.upto(2))
                bank = small(s, "o1", 1)
                if bank is not None:
                    wait(pe, dve_done, s.job(DVE_JOBS, "y1T", 0, 1))
                    pe.matmul(bank[:, 0:D], y1T[s.slot(1, 2)][:], woT[:], start=True, stop=True).then_inc(dve_full, 1)
                bank = small(s, "o2", 3)
                if bank is not None:
                    wait(pe, dve_done, s.job(DVE_JOBS, "y2T", 0, 3))
                    pe.matmul(bank[:, 0:D], y2T[s.slot(3, 2)][:], wpT[:], start=True, stop=True).then_inc(dve_full, 1)

            run(pe, step)

            STEPS = B + LAST
            pe.wait_ge(act_done, STEPS * len(ACT_JOBS))
            pe.wait_ge(dve_done, STEPS * len(DVE_JOBS))
            pe.wait_ge(max_done, B * G)
            TB = [(0, 4), (4, ET)]

            with pe.Fori(0, E // 2) as i:
                for k in range(2):
                    pe.wait_ge(eb_in[k], i * 16 + 16)
                    for n, (c0, c1) in enumerate(TB):
                        pe.wait_ge(t_done, i * 4 + (2 * k) + 1)
                        for c in range(c0, c1):
                            mm = pe.transpose(dve_bank[n][:, (c - c0) * ER:(c - c0 + 1) * ER], EB[k][:, c, :],
                                              ident[0:ER, 0:ER])
                        mm.then_inc(t_full, 1)
                    pe.wait_ge(t_done, i * 4 + (2 * k + 2) + 1)
                    pe.wait_ge(w_in[k], i * 32 + 32)
                    for f in range(FC):
                        for half in range(2):
                            j = 2 * f + half
                            if k == 0 and j < 4:
                                pe.wait_ge(h_done, i * (4 * FC) + 1)
                            else:
                                pe.wait_ge(h_done, i * (4 * FC) + (2 * FC * k + j - 3) + 1)
                            pe.matmul(act_bank[j % 4][:, 0:HALF], w1_sb[k][:, f * P:(f + 1) * P],
                                      ebT[k][:].rearrange("p c r -> p (c r)")[:, half * HALF:(half + 1) * HALF],
                                      start=True, stop=True).then_inc(h_full, 1)
                    pe.wait_ge(h_done, i * (4 * FC) + 2 * FC * (k + 1) + 1)
                    for c in range(ET):
                        n = k * ET + c
                        if n < 2:
                            pe.wait_ge(y_done, i * (2 * ET) + 1)
                        else:
                            pe.wait_ge(y_done, i * (2 * ET) + (n - 1) + 1)
                        for f in range(FC):
                            mm = pe.matmul(max_bank[n % 2][0:ER, 0:D], hT[k][:, f, c * ER:(c + 1) * ER],
                                           w2_sb[k][:, f, :], start=(f == 0), stop=(f == FC - 1))
                        mm.then_inc(y_full, 1)

        @block.scalar
        def _(act):
            def move(s, name, lag, dst, last_read):
                if not s.has(lag):
                    act.drain().then_inc(act_done, 1)
                    return
                wait(act, act_full, s.job(ACT_JOBS, name, 0, lag))
                wait(act, *last_read)
                nc.scalar.copy(dst[:].rearrange("p a t -> p (a t)"), act_slot(s, name, 0, lag)[:]).then_inc(act_done, 1)

            def step(s):
                for u in range(G):
                    if not s.has(1):
                        act.drain().then_inc(act_done, 1)
                        continue
                    wait(act, act_full, s.job(ACT_JOBS, "s1", u, 1))
                    if u == 0:
                        wait(act, dve_full, s.job(DVE_JOBS, "y1", 0, 1, 2))
                    nc.scalar.copy(A1[s.slot(1, 2)][:, u].rearrange("p a t -> p (a t)"),
                                   act_slot(s, "s1", u, 1)[:]).then_inc(act_done, 1)
                move(s, "kx2", 2, KT2[s.slot(2, 2)], (act_full, s.job(ACT_JOBS, "s2t", G - 1, 2, 2)))
                move(s, "qx2", 2, QT2[s.slot(2, 2)], (max_full, s.upto(2, G, 2)))
                if s.has(4):
                    k = s.slot(4, 2)
                    wait(act, logits_ready, s.upto(4))
                    wait(act, slot_ready, s.upto(4, 1, 2))
                    nc.scalar.activation(lexp[:], lg[k][:], ACT.Exp, bias=nlmax[k][:],
                                         accum_out=esum[k][:]).then_inc(esum_ready, 1)
                for u in range(G):
                    if not s.has(3):
                        act.drain().then_inc(act_done, 1)
                        continue
                    wait(act, act_full, s.job(ACT_JOBS, "s2t", u, 3))
                    if u == 0:
                        wait(act, dve_full, s.job(DVE_JOBS, "y2", 0, 3, 2))
                    nc.scalar.activation(P2[s.slot(3, 2)][:, u].rearrange("p a t -> p (a t)"),
                                         act_slot(s, "s2t", u, 3)[:], ACT.Exp, scale=SCALE).then_inc(act_done, 1)
                move(s, "qx", 0, QT[s.slot(0, 2)], (act_full, s.job(ACT_JOBS, "s1", G - 1, 0, 2)))
                move(s, "kx", 0, KT[s.slot(0, 2)], (act_full, s.job(ACT_JOBS, "s1", G - 1, 0, 2)))
                move(s, "qm", 2, QM2[s.slot(2, 2)], (act_full, s.job(ACT_JOBS, "s2t", G - 1, 2, 2)))

            run(act, step)

            with act.Fori(0, E // 2) as i:
                for k in range(2):
                    for f in range(FC):
                        for half in range(2):
                            j = 2 * f + half
                            wait(act, h_full, i * (4 * FC) + (2 * FC * k + j + 1) + 1, passed)
                            if j == 0:
                                wait(act, y_full, i * (2 * ET) + 1, passed)
                            nc.scalar.activation(hT[k][:, f, half * HALF:(half + 1) * HALF],
                                                 act_bank[j % 4][:, 0:HALF], ACT.Gelu,
                                                 bias=b1T[:, bass.ds(i * (2 * FC) + (k * FC + f), 1)]).then_inc(h_done, 1)

        @block.vector
        def _(dve):
            v = nc.vector
            dve.wait_ge(weights_in, 16 * 9)
            dve.wait_ge(setup_full, 1)
            dve.wait_ge(consts, CONSTS)
            v.tensor_copy(wqkvT[:], max_bank[0][:, 0:3 * D])
            v.tensor_copy(woT[:], max_bank[0][:, 3 * D:4 * D])
            v.tensor_copy(wpT[:], max_bank[1][:, 0:D])
            v.tensor_copy(b1T[:], max_bank[1][:, D:D + E * FC])
            v.tensor_scalar(qkvb[:, 0:2 * D], qkvb[:, 0:2 * D], FEATURE_EPS, None, ALU.add).then_inc(setup_done, 1)
            dve.wait_ge(setup_done, 1)
            own = Seq(dve, dve_own, 19, passed)

            def moved(s, name, lag, dst):
                if not s.has(lag):
                    dve.drain().then_inc(dve_done, 1)
                    return
                wait(dve, dve_full, s.job(DVE_JOBS, name, 0, lag))
                v.tensor_copy(dst[:], dve_slot(s, name)[:, 0:P]).then_inc(dve_done, 1)

            def normed(s, name, lag, y, rden, guard, last_read):
                if not s.has(lag):
                    dve.drain().then_inc(dve_done, 1)
                    return
                wait(dve, dve_full, s.job(DVE_JOBS, name, 0, lag))
                wait(dve, dve_full, last_read)
                yd = dve_slot(s, name)[:, 0:H * (HD + 1)].rearrange("p (h d) -> p h d", d=HD + 1)
                if guard is not None:
                    own.mark(v.tensor_scalar(den1[:], yd[:, :, HD], guard, None, ALU.max))
                    own.wait()
                    own.mark(v.reciprocal(rden[:], den1[:]))
                else:
                    own.mark(v.reciprocal(rden[:], yd[:, :, HD]))
                own.wait()
                v.tensor_tensor(y[:], yd[:, :, 0:HD], rden[:].unsqueeze(2).broadcast_to([P, H, HD]),
                                ALU.mult).then_inc(dve_done, 1)
    
            def residual(s, name, lag, r, st, mv, ve, base, ready):
                if not s.has(lag):
                    dve.drain().then_inc(dve_done, 1)
                    return
                wait(dve, dve_full, s.job(DVE_JOBS, name, 0, lag))
                wait(dve, *ready)
                v.tensor_tensor(r[:], dve_slot(s, name)[:, 0:D], base[:], ALU.add).then_inc(dve_done, 1)
                wait(dve, dve_done, s.job(DVE_JOBS, name, 0, lag))
                own.mark(v.bn_stats(st[:], r[:]))
                own.wait(alone=True)
                own.mark(v.bn_aggr(mv[:], st[:]))
                own.wait()

            def step(s):
                moved(s, "xT", 0, xT[s.slot(0, 2)])
                moved(s, "x2T", 4, x2T[s.slot(4, 2)])
                if s.has(0):
                    bank = dve_slot(s, "qkv")
                    wait(dve, dve_full, s.job(DVE_JOBS, "qkv", 0, 0))
                    own.mark(v.tensor_tensor(qkz[:], bank[:, 0:2 * D], qkvb[:, 0:2 * D], ALU.add))
                    wait(dve, dve_full, s.job(DVE_JOBS, "y1", 0, 0, 2))
                    v.tensor_tensor(V1[s.slot(0, 2)][:, :, 0:HD],
                                    bank[:, 2 * D:3 * D].rearrange("p (h d) -> p h d", d=HD),
                                    qkvb[:, 2 * D:3 * D].rearrange("p (h d) -> p h d", d=HD), ALU.add).then_inc(dve_done, 1)
                    own.wait()
                    wait(dve, qkx_ready, s.upto(0, 1, 2))
                    v.tensor_scalar(qk[s.slot(0, 2)][:], qkz[:], FEATURE_EPS, None, ALU.max).then_inc(qk_ready, 1)
                else:
                    dve.drain().then_inc(dve_done, 1)
                if s.has(4):
                    k = s.slot(4, 2)
                    wait(dve, dve_full, s.job(DVE_JOBS, "lg", 0, 4))
                    wait(dve, esum_ready, s.upto(4, 1, 2))
                    v.tensor_copy(lg[k][:], dve_slot(s, "lg")[:, 0:E]).then_inc(dve_done, 1)
                    wait(dve, dve_done, s.job(DVE_JOBS, "lg", 0, 4))
                    own.mark(v.tensor_reduce(lmax[:], lg[k][:], AX_X, ALU.max))
                    own.wait()
                    v.tensor_scalar(nlmax[k][:], lmax[:], -1.0, None, ALU.mult).then_inc(logits_ready, 1)
                    own.mark(v.scalar_tensor_tensor(out=cand[:], in0=lg[k][:], scalar=lmax[:], in1=rank_w[:],
                                                    op0=ALU.is_ge, op1=ALU.mult))
                    own.wait()
                    own.mark(v.tensor_reduce(top[k][:], cand[:], AX_X, ALU.max))
                    own.wait()
                    wait(dve, dve_full, s.job(DVE_JOBS, "rk", 0, 4, 2))
                    v.tensor_scalar(oh[k][:], cand[:], top[k][:], None, ALU.is_equal).then_inc(oh_ready, 1)
                else:
                    dve.drain().then_inc(dve_done, 1)
                if s.has(2):
                    wait(dve, qm_ready, s.upto(2, 1, 2))
                    for u in range(G):
                        wait(dve, max_full, s.upto(2, G, 0, u + 1 - G))
                        v.tensor_reduce(mx[s.slot(2, 2)][:, :, u], max_bank[u % 2][:].rearrange("p (a t) -> p a t", a=NA),
                                        AX_X, ALU.max).then_inc(max_done, 1)
                normed(s, "y1", 1, y1[s.slot(1, 2)], rden1, DEN_EPS, s.job(DVE_JOBS, "y1T", 0, 1, 2))
                normed(s, "y2", 3, y2[s.slot(3, 2)], rden2, None, s.job(DVE_JOBS, "y2T", 0, 3, 2))
                if s.has(4):
                    k, b = s.slot(4, 2), s.batch(4)
                    bank = dve_slot(s, "rk")
                    wait(dve, dve_full, s.job(DVE_JOBS, "rk", 0, 4))
                    wait(dve, oh_ready, s.upto(4))
                    own.mark(v.tensor_tensor(rc[:], bank[:, 0:E], carry[k][:], ALU.add))
                    v.tensor_tensor(carry[1 - k][:], bank[:, E:2 * E], carry[k][:], ALU.add).then_inc(dve_done, 1)
                    own.wait()
                    own.mark(v.tensor_tensor_reduce(rcoh[:], rc[:], oh[k][:], 1.0, 0.0, ALU.mult, ALU.add, rank[:]))
                    own.mark(v.tensor_scalar(slot0[:], top[k][:], -float(CAPP), float(E * CAPP - 1), ALU.mult, ALU.add))
                    own.wait()
                    own.mark(v.tensor_scalar(over[:], rank[:], float(CAP), BIG, ALU.is_gt, ALU.mult))
                    own.mark(v.tensor_tensor(slot1[:], slot0[:], rank[:], ALU.add))
                    own.mark(v.tensor_scalar(valid[:], rank[:], float(CAP), None, ALU.is_le))
                    wait(dve, esum_ready, s.upto(4))
                    own.mark(v.reciprocal(rsum[:], esum[k][:]))
                    own.wait()
                    own.mark(v.tensor_tensor(slot2[:], slot1[:], over[:], ALU.add))
                    v.tensor_tensor(gate_all[:, bass.ds(b, 1)], rsum[:], valid[:], ALU.mult)
                    own.wait()
                    if s.upto(4, 1, 4) is not None:
                        q = (s.n - 4) // 4
                        wait(dve, scattered[s.slot(4, 4)], 16 * q if s.i is None else s.i * 16 + 16 * q)
                    v.tensor_scalar(gidx_all[:, bass.ds(b, 1)], slot2[:], float(TRASH), None, ALU.min)
                    v.tensor_copy(sidx[s.slot(4, 4)][:], slot2[:]).then_inc(slot_ready, 1)
                else:
                    dve.drain().then_inc(dve_done, 1)
                moved(s, "y1T", 1, y1T[s.slot(1, 2)])
                moved(s, "y2T", 3, y2T[s.slot(3, 2)])
                residual(s, "o1", 1, r1, st1, mv1, ve1, xb[s.slot(1, 2)], (xb_ready, s.upto(1)))
                if s.has(1):
                    v.tensor_scalar(ve1[:], mv1[:, 1:2], LN_EPS, None, ALU.add).then_inc(var1_ready, 1)
                residual(s, "o2", 3, r2, st2, mv2, ve2, x1b[s.slot(3, 4)], (qx2_ready, s.upto(3)))
                if s.has(3):
                    v.tensor_scalar(ve2[:], mv2[:, 1:2], LN_EPS, None, ALU.add).then_inc(var2_ready, 1)
                if s.has(1):
                    wait(dve, rstd1_ready, s.upto(1))
                    wait(dve, qx2_ready, s.upto(1, 1, 2))
                    v.tensor_scalar(x1[s.slot(1, 2)][:], r1[:], mv1[:, 0:1], rs1[:], ALU.subtract,
                                    ALU.mult).then_inc(x1_ready, 1)
                if s.has(3):
                    wait(dve, rstd2_ready, s.upto(3))
                    wait(dve, dve_full, s.job(DVE_JOBS, "x2T", 0, 3, 4))
                    wait(dve, x2_kept, s.upto(3, 1, 4))
                    if s.upto(3, 1, 4) is not None:
                        q = (s.n - 3) // 4
                        wait(dve, scattered[s.slot(3, 4)], 16 * q if s.i is None else s.i * 16 + 16 * q)
                    v.tensor_scalar(x2[s.slot(3, 4)][:], r2[:], mv2[:, 0:1], rs2[:], ALU.subtract,
                                    ALU.mult).then_inc(x2_ready, 1)

            run_own(dve, own, step)

            with dve.Fori(0, E // 2) as i:
                for k in range(2):
                    for n, (c0, c1) in enumerate([(0, 4), (4, ET)]):
                        dve.wait_ge(t_full, i * 4 + (2 * k + n + 1))
                        if n == 0:
                            dve.wait_ge(h_full, i * (4 * FC) + 1)
                        v.tensor_copy(ebT[k][:, c0:c1, :].rearrange("p c r -> p (c r)"),
                                      dve_bank[n][:, 0:(c1 - c0) * ER]).then_inc(t_done, 1)
                    for c in range(ET):
                        n = k * ET + c
                        dve.wait_ge(y_full, i * (2 * ET) + (n + 1) + 1)
                        if c == 0:
                            dve.wait_ge(ye_out[k], i * 16 + 16)
                        v.tensor_tensor(yE[k][:, c, :], max_bank[n % 2][0:ER, 0:D],
                                        b2b[0:ER, bass.ds(i * 2 + k, 1), :].rearrange("p o d -> p (o d)"),
                                        ALU.add).then_inc(y_done, 1)

            with dve.Fori(0, B // GR // 2) as i:
                for k in range(2):
                    dve.wait_ge(gathered[k], i * (16 * GR) + 16 * GR)
                    dve.wait_ge(x2_kept, B)
                    for c in range(GR):
                        b = i * (2 * GR) + (k * GR + c)
                        v.scalar_tensor_tensor(out=r3[k][:, c, :], in0=gy[k][:, c, :], scalar=gate_all[:, bass.ds(b, 1)],
                                               in1=x2_all[:, bass.ds(b, 1), :].rearrange("p o d -> p (o d)"),
                                               op0=ALU.mult, op1=ALU.add).then_inc(comb_own, 1)
                    for c in range(GR):
                        dve.wait_ge(comb_own, i * (2 * COMB) + (k * COMB + c + 1))
                        v.bn_stats(st3[:, c, :], r3[k][:, c, :]).then_inc(comb_own, 1)
                    for c in range(GR):
                        wait(dve, comb_own, i * (2 * COMB) + (k * COMB + GR + c + 1), passed)
                        v.bn_aggr(mv3[k][:, c, :], st3[:, c, :]).then_inc(comb_own, 1)
                    dve.wait_ge(comb_own, i * (2 * COMB) + (k + 1) * COMB)
                    v.tensor_scalar(ve3[k][:], mv3[k][:, :, 1], LN_EPS, None, ALU.add).then_inc(var3_ready, 1)
                    dve.wait_ge(rstd3_ready, i * 2 + (k + 1))
                    dve.wait_ge(out_done[k], i * 16 + 16)
                    for c in range(GR):
                        v.tensor_scalar(ot[k][:, c, :], r3[k][:, c, :], mv3[k][:, c, 0:1], rs3[k][:, c:c + 1],
                                        ALU.subtract, ALU.mult).then_inc(ot_ready, 1)


_INS = ['x', 'ctx_1024', 'L0_attn_qkv_w', 'L0_attn_qkv_b', 'L0_attn_out_w', 'L0_attn_out_b',
        'L0_xattn_W_proj', 'L0_xattn_b_proj', 'L0_ffn_wg', 'L0_ffn_W1', 'L0_ffn_b1', 'L0_ffn_W2', 'L0_ffn_b2']


def kernel(**inputs):
    import numpy as _np
    import concourse.bacc as _bacc
    from concourse import mybir as _mybir
    from concourse.bass_utils import run_bass_kernel_spmd as _run

    nc = _bacc.Bacc("TRN2", target_bir_lowering=False, num_devices=1)
    arrays, args = {}, []
    for name in _INS:
        a = _np.ascontiguousarray(inputs[name])
        arrays[f"in_{name}"] = a
        args.append(nc.dram_tensor(f"in_{name}", a.shape, _mybir.dt.from_np(a.dtype), kind="ExternalInput").ap())
    shape = tuple(inputs['x'].shape)
    args.append(nc.dram_tensor("out_x", shape, _mybir.dt.from_np(_np.dtype('float32')), kind="ExternalOutput").ap())
    decoder(nc, *args)
    r = _run(nc, [arrays], core_ids=[0])
    return r.results[0]["out_x"]
```

```python
from contextlib import ExitStack

import concourse.bass as bass
from concourse import mybir

F32 = mybir.dt.float32
F32R = mybir.dt.float32r
BF16 = mybir.dt.bfloat16
U32 = mybir.dt.uint32
ALU = mybir.AluOpType
ACT = mybir.ActivationFunctionType
AX_X = mybir.AxisListType.X

P = 128
UNROLL = 4
FEATURE_EPS = 1e-6
DEN_EPS = 1e-6
LN_EPS = 1e-5
MASKED = -1e30
WINDOW = 64
HALVES = 4

ACT_JOBS = ([("s1", a, 1) for a in range(4)] + [("qx2", 0, 2)] + [("s2t", a, 3) for a in range(4)]
            + [("pv1", 0, 1), ("kx2", 0, 1), ("pv2", 0, 3), ("qx", 0, 0), ("kx", 0, 0), ("qm", 0, 2)])
DVE_JOBS = [("xT", 0, 0), ("x2T", 0, 4), ("qkv", 0, 0), ("lg", 0, 4), ("rk", 0, 4), ("y1", 0, 1),
            ("y1T", 0, 1), ("y2", 0, 3), ("o1", 0, 1), ("y2T", 0, 3), ("o2", 0, 3)]


class Step:

    def __init__(self, n, i=None, batches=32):
        self.n, self.i, self.batches = n, i, batches

    def has(self, lag):
        return 0 <= self.n - lag < self.batches

    def lin(self, value, per_step):
        return value if self.i is None else self.i * (per_step * UNROLL) + value

    def batch(self, lag):
        return self.lin(self.n - lag, 1)

    def slot(self, lag, ring):
        return (self.n - lag) % ring

    def upto(self, lag, per_batch=1, back=0, extra=0):
        if self.n - lag - back < 0:
            return None
        return self.lin((self.n - lag - back + 1) * per_batch + extra, per_batch)

    def landed(self, lag, per_batch, ring, back=0):
        if self.n - lag - back < 0:
            return None
        return self.lin(per_batch * ((self.n - lag - back) // ring + 1), per_batch // ring)

    def job(self, jobs, name, u, lag, back=0):
        at = [k for k, j in enumerate(jobs) if j[0] == name and j[1] == u][0]
        step = self.n - lag - back + jobs[at][2]
        if self.n - lag - back < 0:
            return None
        return self.lin(step * len(jobs) + at + 1, len(jobs))


class Seq:

    def __init__(self, eng, sem, per_step, behind):
        self.eng, self.sem, self.n, self.per_step, self.i, self.behind = eng, sem, 0, per_step, None, behind

    def mark(self, ins):
        self.n += 1
        ins.then_inc(self.sem, 1)
        return self.n

    def wait(self, alone=False):
        n = self.n if self.i is None else self.i * (self.per_step * UNROLL) + self.n
        wait(self.eng, self.sem, n, self.behind if alone else None)


def wait(eng, sem, value, behind=None):
    if sem is None or value is None or (isinstance(value, int) and value <= 0):
        return
    eng.wait_ge(sem, value)
    if behind is not None and not isinstance(value, int):
        eng.sem_inc(behind, 1)


def decoder(nc, x, ctx_in, qkv_w, qkv_b, out_w, out_b, proj_w, proj_b, wg, W1, b1, W2, b2, out):
    B, T, D = x.shape
    E, _, F = W1.shape
    HD = 8
    H = D // HD
    G = P // (HALVES * HD)
    NA = H // G
    VW = HALVES * HD
    SPREAD = 16 * G
    LOADED = 32
    N = B * T
    CAP = int(N / E * 1.25) + 1
    ET = -(-CAP // P)
    ER = -(-CAP // ET)
    CAPP = ER * ET
    TRASH = E * CAPP
    FC = F // P
    HALF = CAPP // 2
    LAST = 4
    LOOP = (2 * UNROLL, B)
    SCALE = float(HD) ** -0.5
    BIG = 1e6
    assert T == P and D == P and CAPP % 2 == 0 and B % UNROLL == 0

    buf = nc.dram_tensor("expert_in", [TRASH, D], F32, kind="Internal").ap()
    ybuf = nc.dram_tensor("expert_out", [TRASH + 1, D], F32, kind="Internal").ap()

    ctx = ExitStack()
    with ctx:
        def sb(name, shape, dt=F32):
            return ctx.enter_context(nc.sbuf_tensor(name, shape, dt))

        def ring(name, n, shape, dt=F32):
            return [sb(f"{name}{k}", shape, dt) for k in range(n)]

        def sem(name):
            return ctx.enter_context(nc.semaphore(name))

        act_bank = [ctx.enter_context(nc.psum_tensor(f"act_bank{k}", [P, 512], F32)) for k in range(4)]
        max_bank = [ctx.enter_context(nc.psum_tensor(f"max_bank{k}", [P, 512], F32)) for k in range(2)]
        dve_bank = [ctx.enter_context(nc.psum_tensor(f"dve_bank{k}", [P, 512], F32)) for k in range(2)]

        ident = sb("ident", [P, P])
        identb = sb("identb", [P, P], BF16)
        upto_t = sb("upto_t", [P, P], BF16)
        onesb = sb("onesb", [P, P], BF16)
        window = sb("window", [P, NA, P], BF16)
        zeros = sb("zeros", [P, TRASH // 4])
        minus_half = sb("minus_half", [P, 4])
        rank_w = sb("rank_w", [P, E])

        w_rows = sb("w_rows", [P, 5, D])
        wqkvT = sb("wqkvT", [P, 3 * D])
        woT = sb("woT", [P, D])
        wpT = sb("wpT", [P, D])
        wg_sb = sb("wg_sb", [P, E])
        b1_rows = sb("b1_rows", [E * FC, P])
        b1T = sb("b1T", [P, E * FC])
        qkvb = sb("qkvb", [P, 3 * D])
        outb = sb("outb", [P, D])
        projb = sb("projb", [P, D])
        b2b = sb("b2b", [P, E, D])

        X = ring("X", 4, [P, D])
        C = ring("C", 4, [P, D])
        xb = ring("xb", 2, [P, D])
        xT = ring("xT", 2, [P, P])
        qk = ring("qk", 2, [P, 2 * D])
        qkz = sb("qkz", [P, 2 * D])
        V1 = ring("V1", 2, [P, H, VW])
        QX = ring("QX", 2, [P, H, HALVES, HD], F32R)
        KX = ring("KX", 2, [P, H, HALVES, HD], F32R)
        QT = ring("QT", 2, [P, NA, P], F32R)
        KT = ring("KT", 2, [P, NA, P], F32R)
        QE = ring("QE", 2, [P, G, NA, P], F32R)
        SC = NA * G * P
        arena = sb("arena", [P, 4 * SC])
        scores = [arena[:, k * SC:(k + 1) * SC].rearrange("p (a j t) -> p a j t", a=NA, j=G) for k in range(4)]
        A1, P2 = scores[0:2], scores[2:4]
        yx1 = sb("yx1", [P, NA, P])
        den1 = sb("den1", [P, H])
        rden1 = sb("rden1", [P, H])
        y1 = ring("y1", 2, [P, H, HD])
        y1T = ring("y1T", 2, [P, P])
        r1 = sb("r1", [P, D])
        st1 = sb("st1", [P, 6])
        mv1 = sb("mv1", [P, 2])
        ve1 = sb("ve1", [P, 1])
        rs1 = sb("rs1", [P, 1])
        x1 = ring("x1", 2, [P, D])
        x1b = ring("x1b", 4, [P, D])
        QX2 = ring("QX2", 2, [P, H, HALVES, HD], F32R)
        KX2 = ring("KX2", 2, [P, H, HALVES, HD], F32R)
        V2 = ring("V2", 4, [P, H, VW])
        QT2 = ring("QT2", 2, [P, NA, P], F32R)
        QM2 = ring("QM2", 2, [P, NA, P], F32R)
        KT2 = ring("KT2", 2, [P, NA, P], F32R)
        mx = ring("mx", 2, [P, H])
        KE2 = ring("KE2", 2, [P, G, NA, P], F32R)
        QME = ring("QME", 2, [P, G, NA, P], F32R)
        yx2 = sb("yx2", [P, NA, P])
        rden2 = sb("rden2", [P, H])
        y2 = ring("y2", 2, [P, H, HD])
        y2T = ring("y2T", 2, [P, P])
        r2 = sb("r2", [P, D])
        st2 = sb("st2", [P, 6])
        mv2 = sb("mv2", [P, 2])
        ve2 = sb("ve2", [P, 1])
        rs2 = sb("rs2", [P, 1])
        x2 = ring("x2", 4, [P, D])
        x2T = ring("x2T", 2, [P, P])
        x2_all = sb("x2_all", [P, B, D])
        lg = ring("lg", 2, [P, E])
        lmax = sb("lmax", [P, 1])
        nlmax = ring("nlmax", 2, [P, 1])
        lexp = sb("lexp", [P, E])
        esum = ring("esum", 2, [P, 1])
        cand = sb("cand", [P, E])
        top = ring("top", 2, [P, 1])
        oh = ring("oh", 2, [P, E], BF16)
        carry = ring("carry", 2, [P, E])
        rc = sb("rc", [P, E])
        rcoh = sb("rcoh", [P, E])
        rank = sb("rank", [P, 1])
        slot0 = sb("slot0", [P, 1])
        slot1 = sb("slot1", [P, 1])
        over = sb("over", [P, 1])
        slot2 = sb("slot2", [P, 1])
        valid = sb("valid", [P, 1])
        rsum = sb("rsum", [P, 1])
        sidx = ring("sidx", 4, [P, 1], U32)
        gidx_all = sb("gidx_all", [P, B], U32)
        gate_all = sb("gate_all", [P, B])
        w1_sb = ring("w1_sb", 2, [P, F])
        w2_sb = ring("w2_sb", 2, [P, FC, D])
        EB = ring("EB", 2, [ER, ET, D])
        def late(at, rows, d0, d1):
            end = at + 2 * d0 * d1
            assert end <= 4 * SC
            return [arena[0:rows, at + k * d0 * d1:at + (k + 1) * d0 * d1].rearrange("p (a b) -> p a b", a=d0)
                    for k in range(2)], end

        ebT, end = late(0, P, ET, ER)
        hT, end = late(end, P, FC, CAPP)
        yE, end = late(end, ER, ET, D)
        GR = 4
        gi = ring("gi", 8, [P, 1], U32)
        gy, end = late(0, P, GR, D)
        r3, end = late(end, P, GR, D)
        st3 = sb("st3", [P, GR, 6])
        mv3 = ring("mv3", 2, [P, GR, 2])
        ve3 = ring("ve3", 2, [P, GR])
        rs3 = ring("rs3", 2, [P, GR])
        ot, end = late(end, P, GR, D)

        weights_in = sem("weights_in")
        zeros_out = sem("zeros_out")
        x_in = [sem(f"x_in{k}") for k in range(4)]
        consts = sem("consts")
        setup_full = sem("setup_full")
        setup_done = sem("setup_done")
        act_full = sem("act_full")
        act_done = sem("act_done")
        max_full = sem("max_full")
        max_done = sem("max_done")
        dve_full = sem("dve_full")
        dve_done = sem("dve_done")
        causal = sem("causal")
        xb_ready = sem("xb_ready")
        qk_ready = sem("qk_ready")
        qkx_ready = sem("qkx_ready")
        kx2_ready = sem("kx2_ready")
        v2_ready = sem("v2_ready")
        spread_zero = sem("spread_zero")
        qe_in = [sem(f"qe_in{k}") for k in range(2)]
        ke_in = [sem(f"ke_in{k}") for k in range(2)]
        qme_in = [sem(f"qme_in{k}") for k in range(2)]
        qx2_ready = sem("qx2_ready")
        qm_ready = sem("qm_ready")
        var1_ready = sem("var1_ready")
        rstd1_ready = sem("rstd1_ready")
        x1_ready = sem("x1_ready")
        x1b_ready = sem("x1b_ready")
        var2_ready = sem("var2_ready")
        rstd2_ready = sem("rstd2_ready")
        x2_ready = sem("x2_ready")
        x2_kept = sem("x2_kept")
        logits_ready = sem("logits_ready")
        esum_ready = sem("esum_ready")
        oh_ready = sem("oh_ready")
        slot_ready = sem("slot_ready")
        scattered = [sem(f"scattered{k}") for k in range(4)]
        dve_own = sem("dve_own")
        pool_own = sem("pool_own")
        w_in = [sem(f"w_in{k}") for k in range(2)]
        eb_in = [sem(f"eb_in{k}") for k in range(2)]
        t_full = sem("t_full")
        t_done = sem("t_done")
        h_full = sem("h_full")
        h_done = sem("h_done")
        y_full = sem("y_full")
        y_done = sem("y_done")
        ye_out = [sem(f"ye_out{k}") for k in range(2)]
        passed = sem("passed")
        gi_ready = sem("gi_ready")
        gathered = [sem(f"gathered{k}") for k in range(2)]
        var3_ready = sem("var3_ready")
        rstd3_ready = sem("rstd3_ready")
        ot_ready = sem("ot_ready")
        comb_own = sem("comb_own")
        out_done = [sem(f"out_done{k}") for k in range(2)]

        CONSTS = 15
        COMB = 3 * GR
        NW = 14
        block = ctx.enter_context(nc.Block())

        def act_slot(s, name, u, lag):
            at = [k for k, j in enumerate(ACT_JOBS) if j[0] == name and j[1] == u][0]
            return act_bank[(s.n * len(ACT_JOBS) + at) % 4]

        def dve_slot(s, name):
            at = [k for k, j in enumerate(DVE_JOBS) if j[0] == name][0]
            return dve_bank[(s.n * len(DVE_JOBS) + at) % 2]

        def lag_of(jobs, name):
            return [j[2] for j in jobs if j[0] == name][0]

        def run(eng, step, loop_end=LOOP[1]):
            for n in range(LOOP[0]):
                step(Step(n))
            with eng.Fori(0, (loop_end - LOOP[0]) // UNROLL) as i:
                for k in range(UNROLL):
                    step(Step(LOOP[0] + k, i))
            for n in range(loop_end, B + LAST):
                step(Step(n))

        def run_own(eng, own, step):
            for n in range(LOOP[0]):
                step(Step(n))
            start = own.n
            with eng.Fori(0, (LOOP[1] - LOOP[0]) // UNROLL) as i:
                own.i = i
                for k in range(UNROLL):
                    step(Step(LOOP[0] + k, i))
            assert own.n - start == own.per_step * UNROLL, (own.n - start, own.per_step)
            own.i = None
            own.n = start + own.per_step * (LOOP[1] - LOOP[0])
            for n in range(LOOP[1], B + LAST):
                step(Step(n))

        @block.sync
        def _(sp):
            def load_batch(b, k):
                sp.dma_start(X[k][:], x[b]).then_inc(x_in[k], 16)
                sp.dma_start(C[k][:], ctx_in[b]).then_inc(x_in[k], 16)

            for count in (t_done, h_full, h_done, y_full, y_done, gi_ready, var3_ready):
                sp.sem_inc(count, 1)
            for k in range(2):
                sp.sem_inc(ye_out[k], 16)
                sp.sem_inc(out_done[k], 16)
            sp.dma_start(w_rows[:, 0:3, :], qkv_w.rearrange("(k p) d -> p k d", p=P)).then_inc(weights_in, 16)
            load_batch(0, 0)
            sp.dma_start(w_rows[:, 3, :], out_w).then_inc(weights_in, 16)
            sp.dma_start(w_rows[:, 4, :], proj_w).then_inc(weights_in, 16)
            sp.dma_start(wg_sb[:], wg).then_inc(weights_in, 16)
            sp.dma_start(b1_rows[:], b1.rearrange("e (k p) -> (e k) p", p=P)).then_inc(weights_in, 16)
            sp.dma_start(qkvb[:], qkv_b.unsqueeze(0).broadcast_to([P, 3 * D])).then_inc(weights_in, 16)
            sp.dma_start(outb[:], out_b.unsqueeze(0).broadcast_to([P, D])).then_inc(weights_in, 16)
            sp.dma_start(projb[:], proj_b.unsqueeze(0).broadcast_to([P, D])).then_inc(weights_in, 16)
            sp.dma_start(b2b[:], b2.unsqueeze(0).broadcast_to([P, E, D])).then_inc(weights_in, 16)
            for k in range(1, 4):
                load_batch(k, k)
            sp.wait_ge(consts, 1)
            zview = buf.rearrange("n d -> (n d)").rearrange("(p f) -> p f", p=P)
            quarter = TRASH // 4
            for k in range(4):
                sp.dma_start(zview[:, k * quarter:(k + 1) * quarter], zeros[:]).then_inc(zeros_out, 16)
            sp.dma_start(ybuf[TRASH:TRASH + 1, :], zeros[0:1, 0:D]).then_inc(zeros_out, 16)

            def spread(s, copy, src, landing, rows):
                for j in range(G):
                    part = slice(VW * j, VW * j + rows)
                    sp.dma_start(copy[part, j].bitcast(F32), src[part].bitcast(F32)).then_inc(landing, 16)

            def step(s):
                if s.has(1):
                    k = s.slot(1, 2)
                    wait(sp, act_done, s.job(ACT_JOBS, "kx2", 0, 1), passed)
                    wait(sp, max_full, s.upto(1, NA, 2), passed)
                    spread(s, KE2[k], KT2[k], ke_in[k], 3 * HD)
                if s.n >= 1 and (s.i is not None or s.n + 3 < B):
                    k = s.slot(-3, 4)
                    wait(sp, dve_full, s.job(DVE_JOBS, "xT", 0, 1), passed)
                    wait(sp, xb_ready, s.upto(1), passed)
                    wait(sp, kx2_ready, s.upto(1), passed)
                    wait(sp, v2_ready, s.upto(1), passed)
                    if s.i is None:
                        load_batch(s.n + 3, k)
                    else:
                        b = s.batch(-3)
                        sp.dma_start(X[k][:], x[bass.ds(b, 1)].rearrange("o t d -> (o t) d")).then_inc(x_in[k], 16)
                        sp.dma_start(C[k][:], ctx_in[bass.ds(b, 1)].rearrange("o t d -> (o t) d")).then_inc(x_in[k], 16)
                if s.has(0):
                    k = s.slot(0, 2)
                    wait(sp, act_done, s.job(ACT_JOBS, "qx", 0, 0), passed)
                    wait(sp, act_full, s.job(ACT_JOBS, "s1", NA - 1, 0, 2), passed)
                    spread(s, QE[k], QT[k], qe_in[k], VW)
                if s.has(2):
                    k = s.slot(2, 2)
                    wait(sp, act_done, s.job(ACT_JOBS, "qm", 0, 2), passed)
                    wait(sp, act_full, s.job(ACT_JOBS, "s2t", NA - 1, 2, 2), passed)
                    spread(s, QME[k], QM2[k], qme_in[k], VW)

            sp.wait_ge(spread_zero, 1)
            run(sp, step, B - UNROLL)

            def expert_rows(e, k, i):
                src = buf[e * CAPP:(e + 1) * CAPP, :] if i is None else buf[bass.ds(i * (2 * CAPP) + k * CAPP, CAPP), :]
                sp.dma_start(EB[k][:], src.rearrange("(c p) d -> p c d", p=ER)).then_inc(eb_in[k], 16)

            def expert_weights(e, k, i):
                w1 = W1[e] if i is None else W1[bass.ds(i * 2 + k, 1)].rearrange("o d f -> (o d) f")
                w2 = W2[e:e + 1] if i is None else W2[bass.ds(i * 2 + k, 1)]
                sp.dma_start(w1_sb[k][:], w1).then_inc(w_in[k], 16)
                sp.dma_start(w2_sb[k][:], w2.rearrange("o (c p) d -> p (o c) d", p=P)).then_inc(w_in[k], 16)

            expert_weights(0, 0, None)
            expert_weights(1, 1, None)
            for k in range(4):
                sp.wait_ge(scattered[k], 16 * (B // 4))
            expert_rows(0, 0, None)
            expert_rows(1, 1, None)

            def store_y(k, i):
                wait(sp, y_done, i * (2 * ET) + (k + 1) * ET + 1, passed)
                dst = ybuf[bass.ds(i * (2 * CAPP) + k * CAPP, CAPP), :]
                sp.dma_start(dst.rearrange("(c p) d -> p c d", p=ER), yE[k][:]).then_inc(ye_out[k], 16)

            with sp.Fori(0, E // 2 - 1) as i:
                for k in range(2):
                    store_y(k, i)
                    wait(sp, y_full, i * (2 * ET) + (k + 1) * ET + 1, passed)
                    w1 = W1[bass.ds(i * 2 + (k + 2), 1)].rearrange("o d f -> (o d) f")
                    w2 = W2[bass.ds(i * 2 + (k + 2), 1)]
                    sp.dma_start(w1_sb[k][:], w1).then_inc(w_in[k], 16)
                    sp.dma_start(w2_sb[k][:], w2.rearrange("o (c p) d -> p (o c) d", p=P)).then_inc(w_in[k], 16)
                    src = buf[bass.ds(i * (2 * CAPP) + (k + 2) * CAPP, CAPP), :]
                    sp.dma_start(EB[k][:], src.rearrange("(c p) d -> p c d", p=ER)).then_inc(eb_in[k], 16)
            for k in range(2):
                e = E - 2 + k
                sp.wait_ge(y_done, (e + 1) * ET + 1)
                sp.dma_start(ybuf[e * CAPP:(e + 1) * CAPP, :].rearrange("(c p) d -> p c d", p=ER),
                             yE[k][:]).then_inc(ye_out[k], 16)

            with sp.Fori(0, B // GR // 2) as i:
                for k in range(2):
                    wait(sp, ot_ready, i * (2 * GR) + (k + 1) * GR, passed)
                    dst = out[bass.ds(i * (2 * GR) + k * GR, GR)]
                    sp.dma_start(dst.rearrange("b t d -> t b d"), ot[k][:]).then_inc(out_done[k], 16)
            for k in range(2):
                sp.wait_ge(out_done[k], 16 * (B // GR // 2) + 16)

        @block.gpsimd
        def _(pool):
            g = nc.gpsimd
            g.memset(zeros[:], 0.0).then_inc(consts, 1)
            g.memset(ident[:], 0.0).then_inc(consts, 1)
            g.memset(identb[:], 0.0).then_inc(consts, 1)
            g.memset(upto_t[:], 1.0).then_inc(consts, 1)
            g.memset(onesb[:], 1.0).then_inc(consts, 1)
            g.memset(window[:], 0.0).then_inc(consts, 1)
            g.memset(minus_half[:], -0.5).then_inc(consts, 1)
            pool.wait_ge(consts, 7)
            diag = dict(pattern=[[-1, P]], channel_multiplier=1, base=0)
            g.affine_select(out=ident[:], in_=ident[:], compare_op=ALU.not_equal, fill=1.0, **diag).then_inc(consts, 1)
            g.affine_select(out=identb[:], in_=identb[:], compare_op=ALU.not_equal, fill=1.0, **diag).then_inc(consts, 1)
            g.affine_select(out=upto_t[:], in_=upto_t[:], compare_op=ALU.is_ge, fill=0.0, base=0,
                            pattern=[[1, P]], channel_multiplier=-1).then_inc(consts, 1)
            g.affine_select(out=window[:], in_=window[:], compare_op=ALU.is_ge, fill=MASKED, base=WINDOW,
                            pattern=[[0, NA], [1, P]], channel_multiplier=-1).then_inc(consts, 1)
            pool.wait_ge(consts, 11)
            g.affine_select(out=window[:], in_=window[:], compare_op=ALU.is_ge, fill=MASKED, base=WINDOW,
                            pattern=[[0, NA], [-1, P]], channel_multiplier=1).then_inc(consts, 1)
            for e in range(E):
                last = g.memset(rank_w[:, e:e + 1], float(E - e))
            last.then_inc(consts, 1)
            for k in range(2):
                g.memset(V1[k][:], 0.0)
                g.memset(QX2[k][:].bitcast(F32), 0.0)
                g.memset(KX2[k][:].bitcast(F32), -1.0)
                g.memset(carry[k][:], 0.0)
            for k in range(4):
                last = g.memset(V2[k][:], 0.0)
            last.then_inc(consts, 1)
            pool.wait_ge(consts, 14)
            for tile in V1 + V2:
                last = g.memset(tile[:, :, HD:HD + 1], 1.0)
            last.then_inc(consts, 1)
            pool.wait_ge(consts, CONSTS)
            pool.wait_ge(weights_in, 16 * 9)
            own = Seq(pool, pool_own, 4, passed)

            def heads(ap):
                return ap.rearrange("p (h d) -> p h d", d=HD)

            def twice(ap):
                return ap.unsqueeze(2).broadcast_to([P, H, 2, HD])

            def step(s):
                if s.has(1):
                    for a in range(NA):
                        wait(pool, act_done, s.job(ACT_JOBS, "s1", a, 1), passed)
                        sc = A1[s.slot(1, 2)][:, a]
                        g.affine_select(out=sc, in_=sc, compare_op=ALU.is_ge, fill=0.0, base=0,
                                        pattern=[[0, G], [1, P]], channel_multiplier=-1).then_inc(causal, 1)
                if s.has(0):
                    k = s.slot(0, 4)
                    wait(pool, x_in[k], s.landed(0, LOADED, 4), passed)
                    wait(pool, var1_ready, s.upto(0, 1, 2), passed)
                    g.tensor_tensor(xb[s.slot(0, 2)][:], X[k][:], outb[:], ALU.add).then_inc(xb_ready, 1)
                if s.has(1):
                    kx, c = KX2[s.slot(1, 2)], heads(C[s.slot(1, 4)][:])
                    wait(pool, act_full, s.job(ACT_JOBS, "kx2", 0, 1, 2), passed)
                    own.mark(g.tensor_copy(kx[:, :, 0:3:2, :], twice(c)))
                    own.wait()
                    g.tensor_tensor(kx[:, :, 1, :], c, kx[:, :, 0, :].bitcast(F32), ALU.subtract).then_inc(kx2_ready, 1)
                if s.has(0):
                    q, kk = heads(qk[s.slot(0, 2)][:, 0:D]), heads(qk[s.slot(0, 2)][:, D:2 * D])
                    qx, kx = QX[s.slot(0, 2)], KX[s.slot(0, 2)]
                    wait(pool, qk_ready, s.upto(0), passed)
                    wait(pool, act_full, s.job(ACT_JOBS, "kx", 0, 0, 2), passed)
                    own.mark(g.tensor_copy(qx[:, :, 0:2, :], twice(q)))
                    own.mark(g.tensor_copy(kx[:, :, 0:4:2, :], twice(kk)))
                    own.wait()
                    g.tensor_tensor(qx[:, :, 2:4, :], twice(q), qx[:, :, 0:2, :].bitcast(F32), ALU.subtract)
                    g.tensor_tensor(kx[:, :, 1:4:2, :], twice(kk), kx[:, :, 0:4:2, :].bitcast(F32),
                                    ALU.subtract).then_inc(qkx_ready, 1)
                if s.has(2):
                    qx = QX2[s.slot(2, 2)][:, :, 3, :]
                    m = mx[s.slot(2, 2)][:].unsqueeze(2)
                    wait(pool, max_done, s.upto(2, NA), passed)
                    wait(pool, act_full, s.job(ACT_JOBS, "qx2", 0, 2), passed)
                    own.mark(g.tensor_copy(qx[:, :, 0:1], m))
                    own.wait()
                    g.tensor_tensor(qx[:, :, 1:2], m, qx[:, :, 0:1].bitcast(F32), ALU.subtract).then_inc(qm_ready, 1)
                if s.has(1):
                    wait(pool, var1_ready, s.upto(1), passed)
                    g.tensor_tensor(rs1[:], ve1[:], minus_half[:, 0:1], ALU.pow).then_inc(rstd1_ready, 1)
                if s.has(1):
                    wait(pool, x1_ready, s.upto(1), passed)
                    wait(pool, var2_ready, s.upto(1, 1, 4), passed)
                    g.tensor_tensor(x1b[s.slot(1, 4)][:], x1[s.slot(1, 2)][:], projb[:], ALU.add).then_inc(x1b_ready, 1)
                if s.has(3):
                    wait(pool, var2_ready, s.upto(3), passed)
                    g.tensor_tensor(rs2[:], ve2[:], minus_half[:, 0:1], ALU.pow).then_inc(rstd2_ready, 1)
                if s.has(4):
                    k = s.slot(4, 4)
                    wait(pool, x2_ready, s.upto(4), passed)
                    wait(pool, slot_ready, s.upto(4), passed)
                    if s.n == 4:
                        pool.wait_ge(zeros_out, 16 * 5)
                    g.indirect_dma_start(out=buf, out_offset=bass.IndirectOffsetOnAxis(ap=sidx[k][:], axis=0),
                                         in_=x2[k][:], in_offset=None, bounds_check=TRASH - 1,
                                         oob_is_err=False).then_inc(scattered[k], 16)

            run_own(pool, own, step)

            pool.wait_ge(zeros_out, 16 * 5)
            for k in range(2):
                pool.wait_ge(ye_out[k], 16 * (E // 2) + 16)
            pool.wait_ge(slot_ready, B)
            with pool.Fori(0, B // GR // 2) as i:
                for k in range(2):
                    wait(pool, gi_ready, i * (2 * GR) + k * GR + 1, passed)
                    wait(pool, var3_ready, i * 2 + 1, passed)
                    for c in range(GR):
                        g.tensor_copy(gi[k * GR + c][:], gidx_all[:, bass.ds(i * (2 * GR) + (k * GR + c), 1)]).then_inc(gi_ready, 1)
                    wait(pool, gi_ready, i * (2 * GR) + (k + 1) * GR + 1, passed)
                    for c in range(GR):
                        g.indirect_dma_start(out=gy[k][:, c, :], out_offset=None, in_=ybuf,
                                             in_offset=bass.IndirectOffsetOnAxis(ap=gi[k * GR + c][:], axis=0),
                                             bounds_check=TRASH, oob_is_err=False).then_inc(gathered[k], 16)
                    wait(pool, var3_ready, i * 2 + (k + 1) + 1, passed)
                    g.tensor_tensor(rs3[k][:], ve3[k][:], minus_half[:, 0:GR], ALU.pow).then_inc(rstd3_ready, 1)

        @block.tensor
        def _(pe):
            pe.wait_ge(consts, CONSTS)
            pe.wait_ge(weights_in, 16 * 9)
            for k in range(4):
                pe.transpose(max_bank[0][:, k * P:(k + 1) * P], w_rows[:, k, :], ident[:])
            pe.transpose(max_bank[1][:, 0:P], w_rows[:, 4, :], ident[:])
            pe.transpose(max_bank[1][:, P:P + E * FC], b1_rows[:], ident[0:E * FC, 0:E * FC]).then_inc(setup_full, 1)
            pe.wait_ge(setup_done, 1)

            def act_take(s, name, u=0):
                at = [k for k, j in enumerate(ACT_JOBS) if j[0] == name and j[1] == u][0]
                n = s.n * len(ACT_JOBS) + at
                if n >= 4:
                    wait(pe, act_done, s.lin(n - 3, len(ACT_JOBS)))
                return act_bank[n % 4]

            def dve_take(s, name):
                at = [k for k, j in enumerate(DVE_JOBS) if j[0] == name][0]
                n = s.n * len(DVE_JOBS) + at
                if n >= 2:
                    wait(pe, dve_done, s.lin(n - 1, len(DVE_JOBS)))
                return dve_bank[n % 2]

            def transposed(s, name, src, lag, ready, value):
                if not s.has(lag):
                    pe.drain().then_inc(act_full, 1)
                    return
                bank = act_take(s, name)
                wait(pe, ready, value)
                for a in range(NA):
                    mm = pe.transpose(bank[:, a * P:(a + 1) * P],
                                      src[:, a * G:(a + 1) * G].rearrange("p j c d -> p (j c d)").bitcast(F32), ident[:])
                mm.then_inc(act_full, 1)

            def small(s, name, lag):
                if not s.has(lag):
                    pe.drain().then_inc(dve_full, 1)
                    return None
                return dve_take(s, name)

            def weighted(s, name, lag, scores, V):
                if not s.has(lag):
                    pe.drain().then_inc(act_full, 1)
                    return
                bank = act_take(s, name)
                for a in range(NA):
                    if name == "pv1":
                        wait(pe, causal, s.upto(lag, NA, 0, a + 1 - NA))
                    else:
                        wait(pe, act_done, s.job(ACT_JOBS, "s2t", a, lag))
                    for j in range(G):
                        mm = pe.matmul(bank[VW * j:VW * (j + 1), a * P:(a + 1) * P], V[:, a * G + j, :],
                                       scores[:, a, j, :], start=True, stop=True, tile_position=(0, VW * j))
                mm.then_inc(act_full, 1)

            def turned(s, name, lag, src, product):
                bank = small(s, name, lag)
                if bank is None:
                    return
                wait(pe, act_done, s.job(ACT_JOBS, product, 0, lag))
                for a in range(NA):
                    mm = pe.transpose(bank[:, a * P:(a + 1) * P], src[:, a, :], ident[:])
                mm.then_inc(dve_full, 1)

            def step(s):
                bank = small(s, "xT", 0)
                if bank is not None:
                    k = s.slot(0, 4)
                    wait(pe, x_in[k], s.landed(0, LOADED, 4))
                    pe.transpose(bank[:, 0:P], X[k][:], ident[:]).then_inc(dve_full, 1)
                bank = small(s, "x2T", 4)
                if bank is not None:
                    wait(pe, x2_ready, s.upto(4))
                    pe.transpose(bank[:, 0:P], x2[s.slot(4, 4)][:], ident[:]).then_inc(dve_full, 1)
                for a in range(NA):
                    if not s.has(1):
                        pe.drain().then_inc(act_full, 1)
                        continue
                    bank = act_take(s, "s1", a)
                    if a == 0:
                        wait(pe, act_done, s.job(ACT_JOBS, "kx", 0, 1))
                        wait(pe, qe_in[s.slot(1, 2)], s.landed(1, SPREAD, 2))
                    pe.matmul(bank[:], KT[s.slot(1, 2)][:, a, :], QE[s.slot(1, 2)][:, :, a, :],
                              start=True, stop=True).then_inc(act_full, 1)
                transposed(s, "qx2", QX2[s.slot(2, 2)], 2, qx2_ready, s.upto(2))
                bank = small(s, "qkv", 0)
                if bank is not None:
                    wait(pe, dve_done, s.job(DVE_JOBS, "xT", 0, 0))
                    pe.matmul(bank[:, 0:3 * D], xT[s.slot(0, 2)][:], wqkvT[:], start=True, stop=True).then_inc(dve_full, 1)
                bank = small(s, "lg", 4)
                if bank is not None:
                    wait(pe, dve_done, s.job(DVE_JOBS, "x2T", 0, 4))
                    pe.matmul(bank[:, 0:E], x2T[s.slot(4, 2)][:], wg_sb[:], start=True, stop=True).then_inc(dve_full, 1)
                for a in range(NA):
                    if not s.has(3):
                        pe.drain().then_inc(act_full, 1)
                        continue
                    bank = act_take(s, "s2t", a)
                    pe.matmul(bank[:], identb[:], window[:].rearrange("p a c -> p (a c)"), start=True, stop=False)
                    if a == 0:
                        wait(pe, act_done, s.job(ACT_JOBS, "kx2", 0, 3))
                        wait(pe, qme_in[s.slot(3, 2)], s.landed(3, SPREAD, 2))
                    pe.matmul(bank[:], KT2[s.slot(3, 2)][:, a, :], QME[s.slot(3, 2)][:, :, a, :],
                              start=False, stop=True).then_inc(act_full, 1)
                if s.has(2):
                    for a in range(NA):
                        if s.n > 2 or a >= 2:
                            wait(pe, max_done, s.upto(2, NA, 0, a - NA - 1))
                        bank = max_bank[a % 2]
                        pe.matmul(bank[:], identb[:], window[:].rearrange("p a c -> p (a c)"), start=True, stop=False)
                        if a == 0:
                            wait(pe, act_done, s.job(ACT_JOBS, "qx2", 0, 2))
                            wait(pe, ke_in[s.slot(2, 2)], s.landed(2, SPREAD, 2))
                        pe.matmul(bank[:], QT2[s.slot(2, 2)][:, a, :], KE2[s.slot(2, 2)][:, :, a, :],
                                  start=False, stop=True).then_inc(max_full, 1)
                bank = small(s, "rk", 4)
                if bank is not None:
                    wait(pe, oh_ready, s.upto(4))
                    pe.matmul(bank[:, 0:E], upto_t[:], oh[s.slot(4, 2)][:], start=True, stop=True)
                    pe.matmul(bank[:, E:2 * E], onesb[:], oh[s.slot(4, 2)][:], start=True, stop=True).then_inc(dve_full, 1)
                weighted(s, "pv1", 1, A1[s.slot(1, 2)], V1[s.slot(1, 2)])
                transposed(s, "kx2", KX2[s.slot(1, 2)], 1, kx2_ready, s.upto(1))
                turned(s, "y1", 1, yx1, "pv1")
                if s.has(3):
                    wait(pe, v2_ready, s.upto(3))
                weighted(s, "pv2", 3, P2[s.slot(3, 2)], V2[s.slot(3, 4)])
                bank = small(s, "y1T", 1)
                if bank is not None:
                    wait(pe, dve_done, s.job(DVE_JOBS, "y1", 0, 1))
                    pe.transpose(bank[:, 0:P], y1[s.slot(1, 2)][:].rearrange("p h d -> p (h d)"), ident[:]).then_inc(dve_full, 1)
                transposed(s, "qx", QX[s.slot(0, 2)], 0, qkx_ready, s.upto(0))
                turned(s, "y2", 3, yx2, "pv2")
                bank = small(s, "o1", 1)
                if bank is not None:
                    wait(pe, dve_done, s.job(DVE_JOBS, "y1T", 0, 1))
                    pe.matmul(bank[:, 0:D], y1T[s.slot(1, 2)][:], woT[:], start=True, stop=True).then_inc(dve_full, 1)
                transposed(s, "kx", KX[s.slot(0, 2)], 0, qkx_ready, s.upto(0))
                bank = small(s, "y2T", 3)
                if bank is not None:
                    wait(pe, dve_done, s.job(DVE_JOBS, "y2", 0, 3))
                    pe.transpose(bank[:, 0:P], y2[s.slot(3, 2)][:].rearrange("p h d -> p (h d)"), ident[:]).then_inc(dve_full, 1)
                transposed(s, "qm", QX2[s.slot(2, 2)], 2, qm_ready, s.upto(2))
                bank = small(s, "o2", 3)
                if bank is not None:
                    wait(pe, dve_done, s.job(DVE_JOBS, "y2T", 0, 3))
                    pe.matmul(bank[:, 0:D], y2T[s.slot(3, 2)][:], wpT[:], start=True, stop=True).then_inc(dve_full, 1)

            run(pe, step)

            STEPS = B + LAST
            pe.wait_ge(act_done, STEPS * len(ACT_JOBS))
            pe.wait_ge(dve_done, STEPS * len(DVE_JOBS))
            pe.wait_ge(max_done, B * G)
            TB = [(0, 4), (4, ET)]

            with pe.Fori(0, E // 2) as i:
                for k in range(2):
                    pe.wait_ge(eb_in[k], i * 16 + 16)
                    for n, (c0, c1) in enumerate(TB):
                        pe.wait_ge(t_done, i * 4 + (2 * k) + 1)
                        for c in range(c0, c1):
                            mm = pe.transpose(dve_bank[n][:, (c - c0) * ER:(c - c0 + 1) * ER], EB[k][:, c, :],
                                              ident[0:ER, 0:ER])
                        mm.then_inc(t_full, 1)
                    pe.wait_ge(t_done, i * 4 + (2 * k + 2) + 1)
                    pe.wait_ge(w_in[k], i * 32 + 32)
                    for f in range(FC):
                        for half in range(2):
                            j = 2 * f + half
                            if k == 0 and j < 4:
                                pe.wait_ge(h_done, i * (4 * FC) + 1)
                            else:
                                pe.wait_ge(h_done, i * (4 * FC) + (2 * FC * k + j - 3) + 1)
                            pe.matmul(act_bank[j % 4][:, 0:HALF], w1_sb[k][:, f * P:(f + 1) * P],
                                      ebT[k][:].rearrange("p c r -> p (c r)")[:, half * HALF:(half + 1) * HALF],
                                      start=True, stop=True).then_inc(h_full, 1)
                    pe.wait_ge(h_done, i * (4 * FC) + 2 * FC * (k + 1) + 1)
                    for c in range(ET):
                        n = k * ET + c
                        if n < 2:
                            pe.wait_ge(y_done, i * (2 * ET) + 1)
                        else:
                            pe.wait_ge(y_done, i * (2 * ET) + (n - 1) + 1)
                        for f in range(FC):
                            mm = pe.matmul(max_bank[n % 2][0:ER, 0:D], hT[k][:, f, c * ER:(c + 1) * ER],
                                           w2_sb[k][:, f, :], start=(f == 0), stop=(f == FC - 1))
                        mm.then_inc(y_full, 1)

        @block.scalar
        def _(act):
            def move(s, name, lag, dst, last_read, copied=(None, None)):
                if not s.has(lag):
                    act.drain().then_inc(act_done, 1)
                    return
                wait(act, act_full, s.job(ACT_JOBS, name, 0, lag))
                wait(act, *last_read)
                wait(act, *copied)
                nc.scalar.copy(dst[:].rearrange("p a t -> p (a t)"), act_slot(s, name, 0, lag)[:]).then_inc(act_done, 1)

            def step(s):
                for a in range(NA):
                    if not s.has(1):
                        act.drain().then_inc(act_done, 1)
                        continue
                    wait(act, act_full, s.job(ACT_JOBS, "s1", a, 1))
                    if a == 0:
                        wait(act, act_full, s.job(ACT_JOBS, "pv1", 0, 1, 2))
                    nc.scalar.copy(A1[s.slot(1, 2)][:, a].rearrange("p j t -> p (j t)"),
                                   act_slot(s, "s1", a, 1)[:]).then_inc(act_done, 1)
                move(s, "qx2", 2, QT2[s.slot(2, 2)], (max_full, s.upto(2, NA, 2)))
                if s.has(4):
                    k = s.slot(4, 2)
                    wait(act, logits_ready, s.upto(4))
                    wait(act, slot_ready, s.upto(4, 1, 2))
                    nc.scalar.activation(lexp[:], lg[k][:], ACT.Exp, bias=nlmax[k][:],
                                         accum_out=esum[k][:]).then_inc(esum_ready, 1)
                for a in range(NA):
                    if not s.has(3):
                        act.drain().then_inc(act_done, 1)
                        continue
                    wait(act, act_full, s.job(ACT_JOBS, "s2t", a, 3))
                    if a == 0:
                        wait(act, act_full, s.job(ACT_JOBS, "pv2", 0, 3, 2))
                    nc.scalar.activation(P2[s.slot(3, 2)][:, a].rearrange("p j t -> p (j t)"),
                                         act_slot(s, "s2t", a, 3)[:], ACT.Exp, scale=SCALE).then_inc(act_done, 1)
                if s.has(4):
                    wait(act, x2_ready, s.upto(4), passed)
                    nc.scalar.copy(x2_all[:, bass.ds(s.batch(4), 1), :].rearrange("p o d -> p (o d)"),
                                   x2[s.slot(4, 4)][:]).then_inc(x2_kept, 1)
                if s.has(1):
                    wait(act, x_in[s.slot(1, 4)], s.landed(1, LOADED, 4))
                    wait(act, act_full, s.job(ACT_JOBS, "pv2", 0, 1, 4))
                    nc.scalar.copy(V2[s.slot(1, 4)][:, :, 0:HD],
                                   C[s.slot(1, 4)][:].rearrange("p (h d) -> p h d", d=HD)).then_inc(v2_ready, 1)
                move(s, "pv1", 1, yx1, (dve_full, s.job(DVE_JOBS, "y1", 0, 1, 1)))
                k = s.slot(1, 2)
                move(s, "kx2", 1, KT2[k], (act_full, s.job(ACT_JOBS, "s2t", NA - 1, 1, 2)),
                     (ke_in[k], s.landed(1, SPREAD, 2, 2)))
                move(s, "pv2", 3, yx2, (dve_full, s.job(DVE_JOBS, "y2", 0, 3, 1)))
                k = s.slot(0, 2)
                move(s, "qx", 0, QT[k], (qe_in[k], s.landed(0, SPREAD, 2, 2)))
                move(s, "kx", 0, KT[k], (act_full, s.job(ACT_JOBS, "s1", NA - 1, 0, 2)))
                k = s.slot(2, 2)
                move(s, "qm", 2, QM2[k], (qme_in[k], s.landed(2, SPREAD, 2, 2)))

            run(act, step)

            with act.Fori(0, E // 2) as i:
                for k in range(2):
                    for f in range(FC):
                        for half in range(2):
                            j = 2 * f + half
                            wait(act, h_full, i * (4 * FC) + (2 * FC * k + j + 1) + 1, passed)
                            if j == 0:
                                wait(act, y_full, i * (2 * ET) + 1, passed)
                            nc.scalar.activation(hT[k][:, f, half * HALF:(half + 1) * HALF],
                                                 act_bank[j % 4][:, 0:HALF], ACT.Gelu,
                                                 bias=b1T[:, bass.ds(i * (2 * FC) + (k * FC + f), 1)]).then_inc(h_done, 1)

        @block.vector
        def _(dve):
            v = nc.vector
            dve.wait_ge(weights_in, 16 * 9)
            dve.wait_ge(setup_full, 1)
            dve.wait_ge(consts, CONSTS)
            v.tensor_copy(wqkvT[:], max_bank[0][:, 0:3 * D])
            v.tensor_copy(woT[:], max_bank[0][:, 3 * D:4 * D])
            v.tensor_copy(wpT[:], max_bank[1][:, 0:D])
            v.tensor_copy(b1T[:], max_bank[1][:, D:D + E * FC])
            v.tensor_scalar(qkvb[:, 0:2 * D], qkvb[:, 0:2 * D], FEATURE_EPS, None, ALU.add).then_inc(setup_done, 1)
            dve.wait_ge(setup_done, 1)
            for tile in QE + KE2 + QME:
                last = v.memset(tile[:].bitcast(F32), 0.0)
            last.then_inc(spread_zero, 1)
            own = Seq(dve, dve_own, 20, passed)

            def moved(s, name, lag, dst):
                if not s.has(lag):
                    dve.drain().then_inc(dve_done, 1)
                    return
                wait(dve, dve_full, s.job(DVE_JOBS, name, 0, lag))
                v.tensor_copy(dst[:], dve_slot(s, name)[:, 0:P]).then_inc(dve_done, 1)

            def normed(s, name, lag, y, rden, guard, last_read):
                if not s.has(lag):
                    dve.drain().then_inc(dve_done, 1)
                    return
                wait(dve, dve_full, s.job(DVE_JOBS, name, 0, lag))
                wait(dve, dve_full, last_read)
                yd = dve_slot(s, name)[:].rearrange("p (h d) -> p h d", d=VW)
                if guard is not None:
                    own.mark(v.tensor_scalar(den1[:], yd[:, :, HD], guard, None, ALU.max))
                    own.wait()
                    own.mark(v.reciprocal(rden[:], den1[:]))
                else:
                    own.mark(v.reciprocal(rden[:], yd[:, :, HD]))
                own.wait()
                v.tensor_tensor(y[:], yd[:, :, 0:HD], rden[:].unsqueeze(2).broadcast_to([P, H, HD]),
                                ALU.mult).then_inc(dve_done, 1)
    
            def residual(s, name, lag, r, st, mv, ve, base, ready):
                if not s.has(lag):
                    dve.drain().then_inc(dve_done, 1)
                    return
                wait(dve, dve_full, s.job(DVE_JOBS, name, 0, lag))
                wait(dve, *ready)
                v.tensor_tensor(r[:], dve_slot(s, name)[:, 0:D], base[:], ALU.add).then_inc(dve_done, 1)
                wait(dve, dve_done, s.job(DVE_JOBS, name, 0, lag))
                own.mark(v.bn_stats(st[:], r[:]))
                own.wait(alone=True)
                own.mark(v.bn_aggr(mv[:], st[:]))
                own.wait()

            def step(s):
                moved(s, "xT", 0, xT[s.slot(0, 2)])
                moved(s, "x2T", 4, x2T[s.slot(4, 2)])
                if s.has(0):
                    bank = dve_slot(s, "qkv")
                    wait(dve, dve_full, s.job(DVE_JOBS, "qkv", 0, 0))
                    own.mark(v.tensor_tensor(qkz[:], bank[:, 0:2 * D], qkvb[:, 0:2 * D], ALU.add))
                    wait(dve, act_full, s.job(ACT_JOBS, "pv1", 0, 0, 2))
                    v.tensor_tensor(V1[s.slot(0, 2)][:, :, 0:HD],
                                    bank[:, 2 * D:3 * D].rearrange("p (h d) -> p h d", d=HD),
                                    qkvb[:, 2 * D:3 * D].rearrange("p (h d) -> p h d", d=HD), ALU.add).then_inc(dve_done, 1)
                    own.wait()
                    wait(dve, qkx_ready, s.upto(0, 1, 2))
                    v.tensor_scalar(qk[s.slot(0, 2)][:], qkz[:], FEATURE_EPS, None, ALU.max).then_inc(qk_ready, 1)
                else:
                    dve.drain().then_inc(dve_done, 1)
                if s.has(4):
                    k = s.slot(4, 2)
                    wait(dve, dve_full, s.job(DVE_JOBS, "lg", 0, 4))
                    wait(dve, esum_ready, s.upto(4, 1, 2))
                    v.tensor_copy(lg[k][:], dve_slot(s, "lg")[:, 0:E]).then_inc(dve_done, 1)
                    wait(dve, dve_done, s.job(DVE_JOBS, "lg", 0, 4))
                    own.mark(v.tensor_reduce(lmax[:], lg[k][:], AX_X, ALU.max))
                    own.wait()
                    v.tensor_scalar(nlmax[k][:], lmax[:], -1.0, None, ALU.mult).then_inc(logits_ready, 1)
                    own.mark(v.scalar_tensor_tensor(out=cand[:], in0=lg[k][:], scalar=lmax[:], in1=rank_w[:],
                                                    op0=ALU.is_ge, op1=ALU.mult))
                    own.wait()
                    own.mark(v.tensor_reduce(top[k][:], cand[:], AX_X, ALU.max))
                    own.wait()
                    wait(dve, dve_full, s.job(DVE_JOBS, "rk", 0, 4, 2))
                    v.tensor_scalar(oh[k][:], cand[:], top[k][:], None, ALU.is_equal).then_inc(oh_ready, 1)
                else:
                    dve.drain().then_inc(dve_done, 1)
                if s.has(2):
                    wait(dve, qm_ready, s.upto(2, 1, 2))
                    for a in range(NA):
                        wait(dve, max_full, s.upto(2, NA, 0, a + 1 - NA))
                        v.tensor_reduce(mx[s.slot(2, 2)][:, a * G:(a + 1) * G],
                                        max_bank[a % 2][:].rearrange("p (j t) -> p j t", j=G),
                                        AX_X, ALU.max).then_inc(max_done, 1)
                if s.has(4):
                    k, b = s.slot(4, 2), s.batch(4)
                    bank = dve_slot(s, "rk")
                    wait(dve, dve_full, s.job(DVE_JOBS, "rk", 0, 4))
                    wait(dve, oh_ready, s.upto(4))
                    own.mark(v.tensor_tensor(rc[:], bank[:, 0:E], carry[k][:], ALU.add))
                    v.tensor_tensor(carry[1 - k][:], bank[:, E:2 * E], carry[k][:], ALU.add).then_inc(dve_done, 1)
                    own.wait()
                    own.mark(v.tensor_tensor_reduce(rcoh[:], rc[:], oh[k][:], 1.0, 0.0, ALU.mult, ALU.add, rank[:]))
                    own.mark(v.tensor_scalar(slot0[:], top[k][:], -float(CAPP), float(E * CAPP - 1), ALU.mult, ALU.add))
                    own.wait()
                    own.mark(v.tensor_scalar(over[:], rank[:], float(CAP), BIG, ALU.is_gt, ALU.mult))
                    own.mark(v.tensor_tensor(slot1[:], slot0[:], rank[:], ALU.add))
                    own.mark(v.tensor_scalar(valid[:], rank[:], float(CAP), None, ALU.is_le))
                    wait(dve, esum_ready, s.upto(4))
                    own.mark(v.reciprocal(rsum[:], esum[k][:]))
                    own.wait()
                    own.mark(v.tensor_tensor(slot2[:], slot1[:], over[:], ALU.add))
                    v.tensor_tensor(gate_all[:, bass.ds(b, 1)], rsum[:], valid[:], ALU.mult)
                    own.wait()
                    if s.upto(4, 1, 4) is not None:
                        q = (s.n - 4) // 4
                        wait(dve, scattered[s.slot(4, 4)], 16 * q if s.i is None else s.i * 16 + 16 * q)
                    v.tensor_scalar(gidx_all[:, bass.ds(b, 1)], slot2[:], float(TRASH), None, ALU.min)
                    v.tensor_copy(sidx[s.slot(4, 4)][:], slot2[:]).then_inc(slot_ready, 1)
                else:
                    dve.drain().then_inc(dve_done, 1)
                normed(s, "y1", 1, y1[s.slot(1, 2)], rden1, DEN_EPS, s.job(DVE_JOBS, "y1T", 0, 1, 2))
                moved(s, "y1T", 1, y1T[s.slot(1, 2)])
                normed(s, "y2", 3, y2[s.slot(3, 2)], rden2, None, s.job(DVE_JOBS, "y2T", 0, 3, 2))
                residual(s, "o1", 1, r1, st1, mv1, ve1, xb[s.slot(1, 2)], (xb_ready, s.upto(1)))
                if s.has(1):
                    v.tensor_scalar(ve1[:], mv1[:, 1:2], LN_EPS, None, ALU.add).then_inc(var1_ready, 1)
                moved(s, "y2T", 3, y2T[s.slot(3, 2)])
                residual(s, "o2", 3, r2, st2, mv2, ve2, x1b[s.slot(3, 4)], (x1b_ready, s.upto(3)))
                if s.has(3):
                    v.tensor_scalar(ve2[:], mv2[:, 1:2], LN_EPS, None, ALU.add).then_inc(var2_ready, 1)
                if s.has(1):
                    wait(dve, rstd1_ready, s.upto(1))
                    wait(dve, x1b_ready, s.upto(1, 1, 2))
                    v.tensor_scalar(x1[s.slot(1, 2)][:], r1[:], mv1[:, 0:1], rs1[:], ALU.subtract,
                                    ALU.mult).then_inc(x1_ready, 1)
                    wait(dve, x1_ready, s.upto(1))
                    wait(dve, act_full, s.job(ACT_JOBS, "qm", 0, 1, 2))
                    xx, qx = x1[s.slot(1, 2)][:].rearrange("p (h d) -> p h d", d=HD), QX2[s.slot(1, 2)]
                    own.mark(v.tensor_copy(qx[:, :, 0:2, :], xx.unsqueeze(2).broadcast_to([P, H, 2, HD])))
                    own.wait()
                    v.tensor_tensor(qx[:, :, 2, :], xx, qx[:, :, 0, :].bitcast(F32), ALU.subtract).then_inc(qx2_ready, 1)
                if s.has(3):
                    wait(dve, rstd2_ready, s.upto(3))
                    wait(dve, dve_full, s.job(DVE_JOBS, "x2T", 0, 3, 4))
                    wait(dve, x2_kept, s.upto(3, 1, 4))
                    if s.upto(3, 1, 4) is not None:
                        q = (s.n - 3) // 4
                        wait(dve, scattered[s.slot(3, 4)], 16 * q if s.i is None else s.i * 16 + 16 * q)
                    v.tensor_scalar(x2[s.slot(3, 4)][:], r2[:], mv2[:, 0:1], rs2[:], ALU.subtract,
                                    ALU.mult).then_inc(x2_ready, 1)

            run_own(dve, own, step)

            with dve.Fori(0, E // 2) as i:
                for k in range(2):
                    for n, (c0, c1) in enumerate([(0, 4), (4, ET)]):
                        dve.wait_ge(t_full, i * 4 + (2 * k + n + 1))
                        if n == 0:
                            dve.wait_ge(h_full, i * (4 * FC) + 1)
                        v.tensor_copy(ebT[k][:, c0:c1, :].rearrange("p c r -> p (c r)"),
                                      dve_bank[n][:, 0:(c1 - c0) * ER]).then_inc(t_done, 1)
                    for c in range(ET):
                        n = k * ET + c
                        dve.wait_ge(y_full, i * (2 * ET) + (n + 1) + 1)
                        if c == 0:
                            dve.wait_ge(ye_out[k], i * 16 + 16)
                        v.tensor_tensor(yE[k][:, c, :], max_bank[n % 2][0:ER, 0:D],
                                        b2b[0:ER, bass.ds(i * 2 + k, 1), :].rearrange("p o d -> p (o d)"),
                                        ALU.add).then_inc(y_done, 1)

            with dve.Fori(0, B // GR // 2) as i:
                for k in range(2):
                    dve.wait_ge(gathered[k], i * (16 * GR) + 16 * GR)
                    dve.wait_ge(x2_kept, B)
                    for c in range(GR):
                        b = i * (2 * GR) + (k * GR + c)
                        v.scalar_tensor_tensor(out=r3[k][:, c, :], in0=gy[k][:, c, :], scalar=gate_all[:, bass.ds(b, 1)],
                                               in1=x2_all[:, bass.ds(b, 1), :].rearrange("p o d -> p (o d)"),
                                               op0=ALU.mult, op1=ALU.add).then_inc(comb_own, 1)
                    for c in range(GR):
                        dve.wait_ge(comb_own, i * (2 * COMB) + (k * COMB + c + 1))
                        v.bn_stats(st3[:, c, :], r3[k][:, c, :]).then_inc(comb_own, 1)
                    for c in range(GR):
                        wait(dve, comb_own, i * (2 * COMB) + (k * COMB + GR + c + 1), passed)
                        v.bn_aggr(mv3[k][:, c, :], st3[:, c, :]).then_inc(comb_own, 1)
                    dve.wait_ge(comb_own, i * (2 * COMB) + (k + 1) * COMB)
                    v.tensor_scalar(ve3[k][:], mv3[k][:, :, 1], LN_EPS, None, ALU.add).then_inc(var3_ready, 1)
                    dve.wait_ge(rstd3_ready, i * 2 + (k + 1))
                    dve.wait_ge(out_done[k], i * 16 + 16)
                    for c in range(GR):
                        v.tensor_scalar(ot[k][:, c, :], r3[k][:, c, :], mv3[k][:, c, 0:1], rs3[k][:, c:c + 1],
                                        ALU.subtract, ALU.mult).then_inc(ot_ready, 1)


_INS = ['x', 'ctx_1024', 'L0_attn_qkv_w', 'L0_attn_qkv_b', 'L0_attn_out_w', 'L0_attn_out_b',
        'L0_xattn_W_proj', 'L0_xattn_b_proj', 'L0_ffn_wg', 'L0_ffn_W1', 'L0_ffn_b1', 'L0_ffn_W2', 'L0_ffn_b2']


def kernel(**inputs):
    import numpy as _np
    import concourse.bacc as _bacc
    from concourse import mybir as _mybir
    from concourse.bass_utils import run_bass_kernel_spmd as _run

    nc = _bacc.Bacc("TRN2", target_bir_lowering=False, num_devices=1)
    arrays, args = {}, []
    for name in _INS:
        a = _np.ascontiguousarray(inputs[name])
        arrays[f"in_{name}"] = a
        args.append(nc.dram_tensor(f"in_{name}", a.shape, _mybir.dt.from_np(a.dtype), kind="ExternalInput").ap())
    shape = tuple(inputs['x'].shape)
    args.append(nc.dram_tensor("out_x", shape, _mybir.dt.from_np(_np.dtype('float32')), kind="ExternalOutput").ap())
    decoder(nc, *args)
    r = _run(nc, [arrays], core_ids=[0])
    return r.results[0]["out_x"]
```

```python
from contextlib import ExitStack

import concourse.bass as bass
from concourse import mybir

F32 = mybir.dt.float32
F32R = mybir.dt.float32r
BF16 = mybir.dt.bfloat16
U32 = mybir.dt.uint32
ALU = mybir.AluOpType
ACT = mybir.ActivationFunctionType
AX_X = mybir.AxisListType.X

P = 128
UNROLL = 4
FEATURE_EPS = 1e-6
DEN_EPS = 1e-6
LN_EPS = 1e-5
MASKED = -1e30
WINDOW = 64
HALVES = 4

ACT_JOBS = ([("s1", a, 1) for a in range(4)] + [("kx2", 0, 1), ("qx2", 0, 2)] + [("s2t", a, 3) for a in range(4)]
            + [("qx", 0, 0), ("kx", 0, 0), ("pv1", 0, 1), ("pv2", 0, 3), ("qm", 0, 2)])
DVE_JOBS = [("xT", 0, 0), ("x2T", 0, 4), ("qkv", 0, 0), ("lg", 0, 4), ("rk", 0, 4), ("y1", 0, 1),
            ("y2", 0, 3), ("y1T", 0, 1), ("y2T", 0, 3), ("o1", 0, 1), ("o2", 0, 3)]


class Step:

    def __init__(self, n, i=None, batches=32):
        self.n, self.i, self.batches = n, i, batches

    def has(self, lag):
        return 0 <= self.n - lag < self.batches

    def lin(self, value, per_step):
        return value if self.i is None else self.i * (per_step * UNROLL) + value

    def batch(self, lag):
        return self.lin(self.n - lag, 1)

    def slot(self, lag, ring):
        return (self.n - lag) % ring

    def upto(self, lag, per_batch=1, back=0, extra=0):
        if self.n - lag - back < 0:
            return None
        return self.lin((self.n - lag - back + 1) * per_batch + extra, per_batch)

    def landed(self, lag, per_batch, ring, back=0):
        if self.n - lag - back < 0:
            return None
        return self.lin(per_batch * ((self.n - lag - back) // ring + 1), per_batch // ring)

    def job(self, jobs, name, u, lag, back=0):
        at = [k for k, j in enumerate(jobs) if j[0] == name and j[1] == u][0]
        step = self.n - lag - back + jobs[at][2]
        if self.n - lag - back < 0:
            return None
        return self.lin(step * len(jobs) + at + 1, len(jobs))


class Seq:

    def __init__(self, eng, sem, per_step, behind):
        self.eng, self.sem, self.n, self.per_step, self.i, self.behind = eng, sem, 0, per_step, None, behind

    def mark(self, ins):
        self.n += 1
        ins.then_inc(self.sem, 1)
        return self.n

    def wait(self, mark=None, alone=False):
        n = self.n if mark is None else mark
        n = n if self.i is None else self.i * (self.per_step * UNROLL) + n
        wait(self.eng, self.sem, n, self.behind if alone else None)


def wait(eng, sem, value, behind=None):
    if sem is None or value is None or (isinstance(value, int) and value <= 0):
        return
    eng.wait_ge(sem, value)
    if behind is not None and not isinstance(value, int):
        eng.sem_inc(behind, 1)


def decoder(nc, x, ctx_in, qkv_w, qkv_b, out_w, out_b, proj_w, proj_b, wg, W1, b1, W2, b2, out):
    B, T, D = x.shape
    E, _, F = W1.shape
    HD = 8
    H = D // HD
    G = P // (HALVES * HD)
    NA = H // G
    VW = HALVES * HD
    SPREAD = 16 * G
    LOADED = 32
    N = B * T
    CAP = int(N / E * 1.25) + 1
    ET = -(-CAP // P)
    ER = -(-CAP // ET)
    CAPP = ER * ET
    TRASH = E * CAPP
    FC = F // P
    HALF = CAPP // 2
    LAST = 4
    LOOP = (2 * UNROLL, B)
    SCALE = float(HD) ** -0.5
    BIG = 1e6
    assert T == P and D == P and CAPP % 2 == 0 and B % UNROLL == 0

    buf = nc.dram_tensor("expert_in", [TRASH, D], F32, kind="Internal").ap()
    ybuf = nc.dram_tensor("expert_out", [TRASH + 1, D], F32, kind="Internal").ap()

    ctx = ExitStack()
    with ctx:
        def sb(name, shape, dt=F32):
            return ctx.enter_context(nc.sbuf_tensor(name, shape, dt))

        def ring(name, n, shape, dt=F32):
            return [sb(f"{name}{k}", shape, dt) for k in range(n)]

        def sem(name):
            return ctx.enter_context(nc.semaphore(name))

        act_bank = [ctx.enter_context(nc.psum_tensor(f"act_bank{k}", [P, 512], F32)) for k in range(4)]
        max_bank = [ctx.enter_context(nc.psum_tensor(f"max_bank{k}", [P, 512], F32)) for k in range(2)]
        dve_bank = [ctx.enter_context(nc.psum_tensor(f"dve_bank{k}", [P, 512], F32)) for k in range(2)]

        ident = sb("ident", [P, P])
        identb = sb("identb", [P, P], BF16)
        upto_t = sb("upto_t", [P, P], BF16)
        onesb = sb("onesb", [P, P], BF16)
        window = sb("window", [P, NA, P], BF16)
        zeros = sb("zeros", [P, TRASH // 4])
        minus_half = sb("minus_half", [P, 4])
        rank_w = sb("rank_w", [P, E])

        w_rows = sb("w_rows", [P, 5, D])
        wqkvT = sb("wqkvT", [P, 3 * D])
        woT = sb("woT", [P, D])
        wpT = sb("wpT", [P, D])
        wg_sb = sb("wg_sb", [P, E])
        b1_rows = sb("b1_rows", [E * FC, P])
        b1T = sb("b1T", [P, E * FC])
        qkvb = sb("qkvb", [P, 3 * D])
        outb = sb("outb", [P, D])
        projb = sb("projb", [P, D])
        b2b = sb("b2b", [P, E, D])

        X = ring("X", 4, [P, D])
        C = ring("C", 4, [P, D])
        xb = ring("xb", 2, [P, D])
        xT = ring("xT", 2, [P, P])
        qk = sb("qk", [P, 2 * D])
        qkz = sb("qkz", [P, 2 * D])
        V1 = ring("V1", 2, [P, H, VW])
        QX = ring("QX", 2, [P, H, HALVES, HD], F32R)
        KX = ring("KX", 2, [P, H, HALVES, HD], F32R)
        QT = ring("QT", 2, [P, NA, P], F32R)
        KT = ring("KT", 2, [P, NA, P], F32R)
        QE = ring("QE", 2, [P, G, NA, P], F32R)
        SC = NA * G * P
        arena = sb("arena", [P, 4 * SC])
        scores = [arena[:, k * SC:(k + 1) * SC].rearrange("p (a j t) -> p a j t", a=NA, j=G) for k in range(4)]
        A1, P2 = scores[0:2], scores[2:4]
        yx1 = sb("yx1", [P, NA, P])
        den1 = sb("den1", [P, H])
        rden1 = sb("rden1", [P, H])
        y1 = ring("y1", 2, [P, H, HD])
        y1T = ring("y1T", 2, [P, P])
        r1 = sb("r1", [P, D])
        st1 = sb("st1", [P, 6])
        mv1 = sb("mv1", [P, 2])
        ve1 = sb("ve1", [P, 1])
        rs1 = sb("rs1", [P, 1])
        x1 = ring("x1", 2, [P, D])
        x1b = ring("x1b", 4, [P, D])
        QX2 = ring("QX2", 2, [P, H, HALVES, HD], F32R)
        KX2 = ring("KX2", 2, [P, H, HALVES, HD], F32R)
        V2 = ring("V2", 4, [P, H, VW])
        QT2 = ring("QT2", 2, [P, NA, P], F32R)
        QM2 = ring("QM2", 2, [P, NA, P], F32R)
        KT2 = ring("KT2", 4, [P, NA, P], F32R)
        mx = ring("mx", 2, [P, H])
        KE2 = ring("KE2", 2, [P, G, NA, P], F32R)
        QME = ring("QME", 2, [P, G, NA, P], F32R)
        yx2 = sb("yx2", [P, NA, P])
        rden2 = sb("rden2", [P, H])
        y2 = ring("y2", 2, [P, H, HD])
        y2T = ring("y2T", 2, [P, P])
        r2 = sb("r2", [P, D])
        st2 = sb("st2", [P, 6])
        mv2 = sb("mv2", [P, 2])
        ve2 = sb("ve2", [P, 1])
        rs2 = sb("rs2", [P, 1])
        x2 = ring("x2", 4, [P, D])
        x2T = ring("x2T", 2, [P, P])
        x2_all = sb("x2_all", [P, B, D])
        lg = ring("lg", 2, [P, E])
        lmax = sb("lmax", [P, 1])
        nlmax = ring("nlmax", 2, [P, 1])
        lexp = sb("lexp", [P, E])
        esum = ring("esum", 2, [P, 1])
        cand = sb("cand", [P, E])
        top = ring("top", 2, [P, 1])
        oh = ring("oh", 2, [P, E], BF16)
        carry = ring("carry", 2, [P, E])
        rc = sb("rc", [P, E])
        rcoh = sb("rcoh", [P, E])
        rank = sb("rank", [P, 1])
        slot0 = sb("slot0", [P, 1])
        slot1 = sb("slot1", [P, 1])
        over = sb("over", [P, 1])
        slot2 = sb("slot2", [P, 1])
        valid = sb("valid", [P, 1])
        rsum = sb("rsum", [P, 1])
        sidx = ring("sidx", 4, [P, 1], U32)
        gidx_all = sb("gidx_all", [P, B], U32)
        gate_all = sb("gate_all", [P, B])
        w1_sb = ring("w1_sb", 2, [P, F])
        w2_sb = ring("w2_sb", 2, [P, FC, D])
        EB = ring("EB", 2, [ER, ET, D])
        def late(at, rows, d0, d1):
            end = at + 2 * d0 * d1
            assert end <= 4 * SC
            return [arena[0:rows, at + k * d0 * d1:at + (k + 1) * d0 * d1].rearrange("p (a b) -> p a b", a=d0)
                    for k in range(2)], end

        ebT, end = late(0, P, ET, ER)
        hT, end = late(end, P, FC, CAPP)
        yE, end = late(end, ER, ET, D)
        GR = 4
        gi = ring("gi", 8, [P, 1], U32)
        gy, end = late(0, P, GR, D)
        r3, end = late(end, P, GR, D)
        st3 = sb("st3", [P, GR, 6])
        mv3 = ring("mv3", 2, [P, GR, 2])
        ve3 = ring("ve3", 2, [P, GR])
        rs3 = ring("rs3", 2, [P, GR])
        ot, end = late(end, P, GR, D)

        weights_in = sem("weights_in")
        zeros_out = sem("zeros_out")
        x_in = [sem(f"x_in{k}") for k in range(4)]
        consts = sem("consts")
        setup_full = sem("setup_full")
        setup_done = sem("setup_done")
        act_full = sem("act_full")
        act_done = sem("act_done")
        max_full = sem("max_full")
        max_done = sem("max_done")
        dve_full = sem("dve_full")
        dve_done = sem("dve_done")
        causal = sem("causal")
        xb_ready = sem("xb_ready")
        qkx_ready = sem("qkx_ready")
        kx2_ready = sem("kx2_ready")
        v2_ready = sem("v2_ready")
        spread_zero = sem("spread_zero")
        qe_in = [sem(f"qe_in{k}") for k in range(2)]
        ke_in = [sem(f"ke_in{k}") for k in range(2)]
        qme_in = [sem(f"qme_in{k}") for k in range(2)]
        qx2_ready = sem("qx2_ready")
        qm_ready = sem("qm_ready")
        var1_ready = sem("var1_ready")
        rstd1_ready = sem("rstd1_ready")
        x1_ready = sem("x1_ready")
        x1b_ready = sem("x1b_ready")
        var2_ready = sem("var2_ready")
        rstd2_ready = sem("rstd2_ready")
        x2_ready = sem("x2_ready")
        x2_kept = sem("x2_kept")
        logits_ready = sem("logits_ready")
        esum_ready = sem("esum_ready")
        oh_ready = sem("oh_ready")
        slot_ready = sem("slot_ready")
        scattered = [sem(f"scattered{k}") for k in range(4)]
        dve_own = sem("dve_own")
        pool_own = sem("pool_own")
        w_in = [sem(f"w_in{k}") for k in range(2)]
        eb_in = [sem(f"eb_in{k}") for k in range(2)]
        t_full = sem("t_full")
        t_done = sem("t_done")
        h_full = sem("h_full")
        h_done = sem("h_done")
        y_full = sem("y_full")
        y_done = sem("y_done")
        ye_out = [sem(f"ye_out{k}") for k in range(2)]
        passed = sem("passed")
        gi_ready = sem("gi_ready")
        gathered = [sem(f"gathered{k}") for k in range(2)]
        var3_ready = sem("var3_ready")
        rstd3_ready = sem("rstd3_ready")
        ot_ready = sem("ot_ready")
        comb_own = sem("comb_own")
        out_done = [sem(f"out_done{k}") for k in range(2)]

        CONSTS = 15
        COMB = 3 * GR
        NW = 14
        block = ctx.enter_context(nc.Block())

        def act_slot(s, name, u, lag):
            at = [k for k, j in enumerate(ACT_JOBS) if j[0] == name and j[1] == u][0]
            return act_bank[(s.n * len(ACT_JOBS) + at) % 4]

        def dve_slot(s, name):
            at = [k for k, j in enumerate(DVE_JOBS) if j[0] == name][0]
            return dve_bank[(s.n * len(DVE_JOBS) + at) % 2]

        def lag_of(jobs, name):
            return [j[2] for j in jobs if j[0] == name][0]

        def run(eng, step, loop_end=LOOP[1]):
            for n in range(LOOP[0]):
                step(Step(n))
            with eng.Fori(0, (loop_end - LOOP[0]) // UNROLL) as i:
                for k in range(UNROLL):
                    step(Step(LOOP[0] + k, i))
            for n in range(loop_end, B + LAST):
                step(Step(n))

        def run_own(eng, own, step):
            for n in range(LOOP[0]):
                step(Step(n))
            start = own.n
            with eng.Fori(0, (LOOP[1] - LOOP[0]) // UNROLL) as i:
                own.i = i
                for k in range(UNROLL):
                    step(Step(LOOP[0] + k, i))
            assert own.n - start == own.per_step * UNROLL, (own.n - start, own.per_step)
            own.i = None
            own.n = start + own.per_step * (LOOP[1] - LOOP[0])
            for n in range(LOOP[1], B + LAST):
                step(Step(n))

        @block.sync
        def _(sp):
            def load_batch(b, k):
                sp.dma_start(X[k][:], x[b]).then_inc(x_in[k], 16)
                sp.dma_start(C[k][:], ctx_in[b]).then_inc(x_in[k], 16)

            for count in (t_done, h_full, h_done, y_full, y_done, gi_ready, var3_ready):
                sp.sem_inc(count, 1)
            for k in range(2):
                sp.sem_inc(ye_out[k], 16)
                sp.sem_inc(out_done[k], 16)
            sp.dma_start(w_rows[:, 0:3, :], qkv_w.rearrange("(k p) d -> p k d", p=P)).then_inc(weights_in, 16)
            load_batch(0, 0)
            sp.dma_start(w_rows[:, 3, :], out_w).then_inc(weights_in, 16)
            sp.dma_start(w_rows[:, 4, :], proj_w).then_inc(weights_in, 16)
            sp.dma_start(wg_sb[:], wg).then_inc(weights_in, 16)
            sp.dma_start(b1_rows[:], b1.rearrange("e (k p) -> (e k) p", p=P)).then_inc(weights_in, 16)
            sp.dma_start(qkvb[:], qkv_b.unsqueeze(0).broadcast_to([P, 3 * D])).then_inc(weights_in, 16)
            sp.dma_start(outb[:], out_b.unsqueeze(0).broadcast_to([P, D])).then_inc(weights_in, 16)
            sp.dma_start(projb[:], proj_b.unsqueeze(0).broadcast_to([P, D])).then_inc(weights_in, 16)
            sp.dma_start(b2b[:], b2.unsqueeze(0).broadcast_to([P, E, D])).then_inc(weights_in, 16)
            for k in range(1, 4):
                load_batch(k, k)
            sp.wait_ge(consts, 1)
            zview = buf.rearrange("n d -> (n d)").rearrange("(p f) -> p f", p=P)
            quarter = TRASH // 4
            for k in range(4):
                sp.dma_start(zview[:, k * quarter:(k + 1) * quarter], zeros[:]).then_inc(zeros_out, 16)
            sp.dma_start(ybuf[TRASH:TRASH + 1, :], zeros[0:1, 0:D]).then_inc(zeros_out, 16)

            def spread(s, copy, src, landing, rows):
                for j in range(G):
                    part = slice(VW * j, VW * j + rows)
                    sp.dma_start(copy[part, j].bitcast(F32), src[part].bitcast(F32)).then_inc(landing, 16)

            def step(s):
                if s.has(1):
                    k = s.slot(1, 2)
                    wait(sp, act_done, s.job(ACT_JOBS, "kx2", 0, 1), passed)
                    wait(sp, max_full, s.upto(1, NA, 2), passed)
                    spread(s, KE2[k], KT2[s.slot(1, 4)], ke_in[k], 3 * HD)
                if s.n >= 1 and (s.i is not None or s.n + 3 < B):
                    k = s.slot(-3, 4)
                    wait(sp, dve_full, s.job(DVE_JOBS, "xT", 0, 1), passed)
                    wait(sp, xb_ready, s.upto(1), passed)
                    wait(sp, kx2_ready, s.upto(1), passed)
                    wait(sp, v2_ready, s.upto(1), passed)
                    if s.i is None:
                        load_batch(s.n + 3, k)
                    else:
                        b = s.batch(-3)
                        sp.dma_start(X[k][:], x[bass.ds(b, 1)].rearrange("o t d -> (o t) d")).then_inc(x_in[k], 16)
                        sp.dma_start(C[k][:], ctx_in[bass.ds(b, 1)].rearrange("o t d -> (o t) d")).then_inc(x_in[k], 16)
                if s.has(0):
                    k = s.slot(0, 2)
                    wait(sp, act_done, s.job(ACT_JOBS, "qx", 0, 0), passed)
                    wait(sp, act_full, s.job(ACT_JOBS, "s1", NA - 1, 0, 2), passed)
                    spread(s, QE[k], QT[k], qe_in[k], VW)
                if s.has(2):
                    k = s.slot(2, 2)
                    wait(sp, act_done, s.job(ACT_JOBS, "qm", 0, 2), passed)
                    wait(sp, act_full, s.job(ACT_JOBS, "s2t", NA - 1, 2, 2), passed)
                    spread(s, QME[k], QM2[k], qme_in[k], VW)

            sp.wait_ge(spread_zero, 1)
            run(sp, step, B - UNROLL)

            def expert_rows(e, k, i):
                src = buf[e * CAPP:(e + 1) * CAPP, :] if i is None else buf[bass.ds(i * (2 * CAPP) + k * CAPP, CAPP), :]
                sp.dma_start(EB[k][:], src.rearrange("(c p) d -> p c d", p=ER)).then_inc(eb_in[k], 16)

            def expert_weights(e, k, i):
                w1 = W1[e] if i is None else W1[bass.ds(i * 2 + k, 1)].rearrange("o d f -> (o d) f")
                w2 = W2[e:e + 1] if i is None else W2[bass.ds(i * 2 + k, 1)]
                sp.dma_start(w1_sb[k][:], w1).then_inc(w_in[k], 16)
                sp.dma_start(w2_sb[k][:], w2.rearrange("o (c p) d -> p (o c) d", p=P)).then_inc(w_in[k], 16)

            expert_weights(0, 0, None)
            expert_weights(1, 1, None)
            for k in range(4):
                sp.wait_ge(scattered[k], 16 * (B // 4))
            expert_rows(0, 0, None)
            expert_rows(1, 1, None)

            def store_y(k, i):
                wait(sp, y_done, i * (2 * ET) + (k + 1) * ET + 1, passed)
                dst = ybuf[bass.ds(i * (2 * CAPP) + k * CAPP, CAPP), :]
                sp.dma_start(dst.rearrange("(c p) d -> p c d", p=ER), yE[k][:]).then_inc(ye_out[k], 16)

            with sp.Fori(0, E // 2 - 1) as i:
                for k in range(2):
                    store_y(k, i)
                    wait(sp, y_full, i * (2 * ET) + (k + 1) * ET + 1, passed)
                    w1 = W1[bass.ds(i * 2 + (k + 2), 1)].rearrange("o d f -> (o d) f")
                    w2 = W2[bass.ds(i * 2 + (k + 2), 1)]
                    sp.dma_start(w1_sb[k][:], w1).then_inc(w_in[k], 16)
                    sp.dma_start(w2_sb[k][:], w2.rearrange("o (c p) d -> p (o c) d", p=P)).then_inc(w_in[k], 16)
                    src = buf[bass.ds(i * (2 * CAPP) + (k + 2) * CAPP, CAPP), :]
                    sp.dma_start(EB[k][:], src.rearrange("(c p) d -> p c d", p=ER)).then_inc(eb_in[k], 16)
            for k in range(2):
                e = E - 2 + k
                sp.wait_ge(y_done, (e + 1) * ET + 1)
                sp.dma_start(ybuf[e * CAPP:(e + 1) * CAPP, :].rearrange("(c p) d -> p c d", p=ER),
                             yE[k][:]).then_inc(ye_out[k], 16)

            with sp.Fori(0, B // GR // 2) as i:
                for k in range(2):
                    wait(sp, ot_ready, i * (2 * GR) + (k + 1) * GR, passed)
                    dst = out[bass.ds(i * (2 * GR) + k * GR, GR)]
                    sp.dma_start(dst.rearrange("b t d -> t b d"), ot[k][:]).then_inc(out_done[k], 16)
            for k in range(2):
                sp.wait_ge(out_done[k], 16 * (B // GR // 2) + 16)

        @block.gpsimd
        def _(pool):
            g = nc.gpsimd
            g.memset(zeros[:], 0.0).then_inc(consts, 1)
            g.memset(ident[:], 0.0).then_inc(consts, 1)
            g.memset(identb[:], 0.0).then_inc(consts, 1)
            g.memset(upto_t[:], 1.0).then_inc(consts, 1)
            g.memset(onesb[:], 1.0).then_inc(consts, 1)
            g.memset(window[:], 0.0).then_inc(consts, 1)
            g.memset(minus_half[:], -0.5).then_inc(consts, 1)
            pool.wait_ge(consts, 7)
            diag = dict(pattern=[[-1, P]], channel_multiplier=1, base=0)
            g.affine_select(out=ident[:], in_=ident[:], compare_op=ALU.not_equal, fill=1.0, **diag).then_inc(consts, 1)
            g.affine_select(out=identb[:], in_=identb[:], compare_op=ALU.not_equal, fill=1.0, **diag).then_inc(consts, 1)
            g.affine_select(out=upto_t[:], in_=upto_t[:], compare_op=ALU.is_ge, fill=0.0, base=0,
                            pattern=[[1, P]], channel_multiplier=-1).then_inc(consts, 1)
            g.affine_select(out=window[:], in_=window[:], compare_op=ALU.is_ge, fill=MASKED, base=WINDOW,
                            pattern=[[0, NA], [1, P]], channel_multiplier=-1).then_inc(consts, 1)
            pool.wait_ge(consts, 11)
            g.affine_select(out=window[:], in_=window[:], compare_op=ALU.is_ge, fill=MASKED, base=WINDOW,
                            pattern=[[0, NA], [-1, P]], channel_multiplier=1).then_inc(consts, 1)
            for e in range(E):
                last = g.memset(rank_w[:, e:e + 1], float(E - e))
            last.then_inc(consts, 1)
            for k in range(2):
                g.memset(V1[k][:], 0.0)
                g.memset(QX2[k][:].bitcast(F32), 0.0)
                g.memset(KX2[k][:].bitcast(F32), -1.0)
                g.memset(carry[k][:], 0.0)
            for k in range(4):
                last = g.memset(V2[k][:], 0.0)
            last.then_inc(consts, 1)
            pool.wait_ge(consts, 14)
            for tile in V1 + V2:
                last = g.memset(tile[:, :, HD:HD + 1], 1.0)
            last.then_inc(consts, 1)
            pool.wait_ge(consts, CONSTS)
            pool.wait_ge(weights_in, 16 * 9)
            own = Seq(pool, pool_own, 2, passed)

            def heads(ap):
                return ap.rearrange("p (h d) -> p h d", d=HD)

            def twice(ap):
                return ap.unsqueeze(2).broadcast_to([P, H, 2, HD])

            def step(s):
                if s.has(2):
                    wait(pool, x1_ready, s.upto(2), passed)
                    wait(pool, var2_ready, s.upto(2, 1, 4), passed)
                    g.tensor_tensor(x1b[s.slot(2, 4)][:], x1[s.slot(2, 2)][:], projb[:], ALU.add).then_inc(x1b_ready, 1)
                if s.has(1):
                    for a in range(NA):
                        wait(pool, act_done, s.job(ACT_JOBS, "s1", a, 1), passed)
                        sc = A1[s.slot(1, 2)][:, a]
                        g.affine_select(out=sc, in_=sc, compare_op=ALU.is_ge, fill=0.0, base=0,
                                        pattern=[[0, G], [1, P]], channel_multiplier=-1).then_inc(causal, 1)
                if s.has(0):
                    k = s.slot(0, 4)
                    wait(pool, x_in[k], s.landed(0, LOADED, 4), passed)
                    wait(pool, var1_ready, s.upto(0, 1, 2), passed)
                    g.tensor_tensor(xb[s.slot(0, 2)][:], X[k][:], outb[:], ALU.add).then_inc(xb_ready, 1)
                if s.has(0):
                    kx, c = KX2[s.slot(0, 2)], heads(C[s.slot(0, 4)][:])
                    wait(pool, act_full, s.job(ACT_JOBS, "kx2", 0, 0, 2), passed)
                    own.mark(g.tensor_copy(kx[:, :, 0:3:2, :], twice(c)))
                    own.wait()
                    g.tensor_tensor(kx[:, :, 1, :], c, kx[:, :, 0, :].bitcast(F32), ALU.subtract).then_inc(kx2_ready, 1)
                if s.has(2):
                    qx = QX2[s.slot(2, 2)][:, :, 3, :]
                    m = mx[s.slot(2, 2)][:].unsqueeze(2)
                    wait(pool, max_done, s.upto(2, NA), passed)
                    wait(pool, act_full, s.job(ACT_JOBS, "qx2", 0, 2), passed)
                    own.mark(g.tensor_copy(qx[:, :, 0:1], m))
                    own.wait()
                    g.tensor_tensor(qx[:, :, 1:2], m, qx[:, :, 0:1].bitcast(F32), ALU.subtract).then_inc(qm_ready, 1)
                if s.has(4):
                    k = s.slot(4, 4)
                    wait(pool, x2_ready, s.upto(4), passed)
                    wait(pool, slot_ready, s.upto(4), passed)
                    if s.n == 4:
                        pool.wait_ge(zeros_out, 16 * 5)
                    g.indirect_dma_start(out=buf, out_offset=bass.IndirectOffsetOnAxis(ap=sidx[k][:], axis=0),
                                         in_=x2[k][:], in_offset=None, bounds_check=TRASH - 1,
                                         oob_is_err=False).then_inc(scattered[k], 16)
                if s.has(1):
                    wait(pool, var1_ready, s.upto(1), passed)
                    g.tensor_tensor(rs1[:], ve1[:], minus_half[:, 0:1], ALU.pow).then_inc(rstd1_ready, 1)
                if s.has(3):
                    wait(pool, var2_ready, s.upto(3), passed)
                    g.tensor_tensor(rs2[:], ve2[:], minus_half[:, 0:1], ALU.pow).then_inc(rstd2_ready, 1)

            run_own(pool, own, step)

            pool.wait_ge(zeros_out, 16 * 5)
            for k in range(2):
                pool.wait_ge(ye_out[k], 16 * (E // 2) + 16)
            pool.wait_ge(slot_ready, B)

            def at(i, per_pass, first):
                return first if i is None else i * per_pass + first

            def gather(n, i=None):
                k = n % 2
                if n > 0:
                    wait(pool, var3_ready, at(i, 2, n), passed)
                for c in range(GR):
                    g.tensor_copy(gi[k * GR + c][:],
                                  gidx_all[:, bass.ds(at(i, 2 * GR, n * GR + c), 1)]).then_inc(gi_ready, 1)
                for c in range(GR):
                    wait(pool, gi_ready, at(i, 2 * GR, n * GR + c + 2), passed)
                    g.indirect_dma_start(out=gy[k][:, c, :], out_offset=None, in_=ybuf,
                                         in_offset=bass.IndirectOffsetOnAxis(ap=gi[k * GR + c][:], axis=0),
                                         bounds_check=TRASH, oob_is_err=False).then_inc(gathered[k], 16)

            def root(n, i=None):
                k = n % 2
                wait(pool, var3_ready, at(i, 2, n + 2), passed)
                g.tensor_tensor(rs3[k][:], ve3[k][:], minus_half[:, 0:GR], ALU.pow).then_inc(rstd3_ready, 1)

            GROUPS = B // GR
            gather(0)
            with pool.Fori(0, GROUPS // 2 - 1) as i:
                for n in range(2):
                    gather(n + 1, i)
                    root(n, i)
            gather(GROUPS - 1)
            root(GROUPS - 2)
            root(GROUPS - 1)

        @block.tensor
        def _(pe):
            pe.wait_ge(consts, CONSTS)
            pe.wait_ge(weights_in, 16 * 9)
            for k in range(4):
                pe.transpose(max_bank[0][:, k * P:(k + 1) * P], w_rows[:, k, :], ident[:])
            pe.transpose(max_bank[1][:, 0:P], w_rows[:, 4, :], ident[:])
            pe.transpose(max_bank[1][:, P:P + E * FC], b1_rows[:], ident[0:E * FC, 0:E * FC]).then_inc(setup_full, 1)
            pe.wait_ge(setup_done, 1)

            def act_take(s, name, u=0):
                at = [k for k, j in enumerate(ACT_JOBS) if j[0] == name and j[1] == u][0]
                n = s.n * len(ACT_JOBS) + at
                if n >= 4:
                    wait(pe, act_done, s.lin(n - 3, len(ACT_JOBS)))
                return act_bank[n % 4]

            def dve_take(s, name):
                at = [k for k, j in enumerate(DVE_JOBS) if j[0] == name][0]
                n = s.n * len(DVE_JOBS) + at
                if n >= 2:
                    wait(pe, dve_done, s.lin(n - 1, len(DVE_JOBS)))
                return dve_bank[n % 2]

            def transposed(s, name, src, lag, ready, value):
                if not s.has(lag):
                    pe.drain().then_inc(act_full, 1)
                    return
                bank = act_take(s, name)
                wait(pe, ready, value)
                for a in range(NA):
                    mm = pe.transpose(bank[:, a * P:(a + 1) * P],
                                      src[:, a * G:(a + 1) * G].rearrange("p j c d -> p (j c d)").bitcast(F32), ident[:])
                mm.then_inc(act_full, 1)

            def small(s, name, lag):
                if not s.has(lag):
                    pe.drain().then_inc(dve_full, 1)
                    return None
                return dve_take(s, name)

            def weighted(s, name, lag, scores, V):
                if not s.has(lag):
                    pe.drain().then_inc(act_full, 1)
                    return
                bank = act_take(s, name)
                for a in range(NA):
                    if name == "pv1":
                        wait(pe, causal, s.upto(lag, NA, 0, a + 1 - NA))
                    else:
                        wait(pe, act_done, s.job(ACT_JOBS, "s2t", a, lag))
                    for j in range(G):
                        mm = pe.matmul(bank[VW * j:VW * (j + 1), a * P:(a + 1) * P], V[:, a * G + j, :],
                                       scores[:, a, j, :], start=True, stop=True, tile_position=(0, VW * j))
                mm.then_inc(act_full, 1)

            def maxima(s, groups):
                if not s.has(2):
                    return
                for a in groups:
                    if s.n > 2 or a >= 2:
                        wait(pe, max_done, s.upto(2, NA, 0, a - NA - 1))
                    bank = max_bank[a % 2]
                    pe.matmul(bank[:], identb[:], window[:].rearrange("p a c -> p (a c)"), start=True, stop=False)
                    if a == 0:
                        wait(pe, act_done, s.job(ACT_JOBS, "qx2", 0, 2))
                        wait(pe, ke_in[s.slot(2, 2)], s.landed(2, SPREAD, 2))
                    pe.matmul(bank[:], QT2[s.slot(2, 2)][:, a, :], KE2[s.slot(2, 2)][:, :, a, :],
                              start=False, stop=True).then_inc(max_full, 1)

            def turned(s, name, lag, src, product):
                bank = small(s, name, lag)
                if bank is None:
                    return
                wait(pe, act_done, s.job(ACT_JOBS, product, 0, lag))
                for a in range(NA):
                    mm = pe.transpose(bank[:, a * P:(a + 1) * P], src[:, a, :], ident[:])
                mm.then_inc(dve_full, 1)

            def step(s):
                bank = small(s, "xT", 0)
                if bank is not None:
                    k = s.slot(0, 4)
                    wait(pe, x_in[k], s.landed(0, LOADED, 4))
                    pe.transpose(bank[:, 0:P], X[k][:], ident[:]).then_inc(dve_full, 1)
                for a in range(NA):
                    if not s.has(1):
                        pe.drain().then_inc(act_full, 1)
                        continue
                    bank = act_take(s, "s1", a)
                    if a == 0:
                        wait(pe, act_done, s.job(ACT_JOBS, "kx", 0, 1))
                        wait(pe, qe_in[s.slot(1, 2)], s.landed(1, SPREAD, 2))
                    pe.matmul(bank[:], KT[s.slot(1, 2)][:, a, :], QE[s.slot(1, 2)][:, :, a, :],
                              start=True, stop=True).then_inc(act_full, 1)
                transposed(s, "kx2", KX2[s.slot(1, 2)], 1, kx2_ready, s.upto(1))
                transposed(s, "qx2", QX2[s.slot(2, 2)], 2, qx2_ready, s.upto(2))
                bank = small(s, "x2T", 4)
                if bank is not None:
                    wait(pe, x2_ready, s.upto(4))
                    pe.transpose(bank[:, 0:P], x2[s.slot(4, 4)][:], ident[:]).then_inc(dve_full, 1)
                bank = small(s, "qkv", 0)
                if bank is not None:
                    wait(pe, dve_done, s.job(DVE_JOBS, "xT", 0, 0))
                    pe.matmul(bank[:, 0:3 * D], xT[s.slot(0, 2)][:], wqkvT[:], start=True, stop=True).then_inc(dve_full, 1)
                bank = small(s, "lg", 4)
                if bank is not None:
                    wait(pe, dve_done, s.job(DVE_JOBS, "x2T", 0, 4))
                    pe.matmul(bank[:, 0:E], x2T[s.slot(4, 2)][:], wg_sb[:], start=True, stop=True).then_inc(dve_full, 1)
                for a in range(NA):
                    if not s.has(3):
                        pe.drain().then_inc(act_full, 1)
                        continue
                    bank = act_take(s, "s2t", a)
                    pe.matmul(bank[:], identb[:], window[:].rearrange("p a c -> p (a c)"), start=True, stop=False)
                    if a == 0:
                        wait(pe, act_done, s.job(ACT_JOBS, "kx2", 0, 3))
                        wait(pe, qme_in[s.slot(3, 2)], s.landed(3, SPREAD, 2))
                    pe.matmul(bank[:], KT2[s.slot(3, 4)][:, a, :], QME[s.slot(3, 2)][:, :, a, :],
                              start=False, stop=True).then_inc(act_full, 1)
                maxima(s, (0, 1))
                transposed(s, "qx", QX[s.slot(0, 2)], 0, qkx_ready, s.upto(0))
                transposed(s, "kx", KX[s.slot(0, 2)], 0, qkx_ready, s.upto(0))
                weighted(s, "pv1", 1, A1[s.slot(1, 2)], V1[s.slot(1, 2)])
                maxima(s, (2,))
                bank = small(s, "rk", 4)
                if bank is not None:
                    wait(pe, oh_ready, s.upto(4))
                    pe.matmul(bank[:, 0:E], upto_t[:], oh[s.slot(4, 2)][:], start=True, stop=True)
                    pe.matmul(bank[:, E:2 * E], onesb[:], oh[s.slot(4, 2)][:], start=True, stop=True).then_inc(dve_full, 1)
                maxima(s, (3,))
                if s.has(3):
                    wait(pe, v2_ready, s.upto(3))
                weighted(s, "pv2", 3, P2[s.slot(3, 2)], V2[s.slot(3, 4)])
                turned(s, "y1", 1, yx1, "pv1")
                turned(s, "y2", 3, yx2, "pv2")
                transposed(s, "qm", QX2[s.slot(2, 2)], 2, qm_ready, s.upto(2))
                for name, lag, product, y in (("y1T", 1, "y1", y1), ("y2T", 3, "y2", y2)):
                    bank = small(s, name, lag)
                    if bank is not None:
                        wait(pe, dve_done, s.job(DVE_JOBS, product, 0, lag))
                        pe.transpose(bank[:, 0:P], y[s.slot(lag, 2)][:].rearrange("p h d -> p (h d)"),
                                     ident[:]).then_inc(dve_full, 1)
                for name, lag, product, yT, w in (("o1", 1, "y1T", y1T, woT), ("o2", 3, "y2T", y2T, wpT)):
                    bank = small(s, name, lag)
                    if bank is not None:
                        wait(pe, dve_done, s.job(DVE_JOBS, product, 0, lag))
                        pe.matmul(bank[:, 0:D], yT[s.slot(lag, 2)][:], w[:], start=True, stop=True).then_inc(dve_full, 1)

            run(pe, step)

            STEPS = B + LAST
            pe.wait_ge(act_done, STEPS * len(ACT_JOBS))
            pe.wait_ge(dve_done, STEPS * len(DVE_JOBS))
            pe.wait_ge(max_done, B * G)
            TB = [(0, 4), (4, ET)]

            with pe.Fori(0, E // 2) as i:
                for k in range(2):
                    pe.wait_ge(eb_in[k], i * 16 + 16)
                    for n, (c0, c1) in enumerate(TB):
                        pe.wait_ge(t_done, i * 4 + (2 * k) + 1)
                        for c in range(c0, c1):
                            mm = pe.transpose(dve_bank[n][:, (c - c0) * ER:(c - c0 + 1) * ER], EB[k][:, c, :],
                                              ident[0:ER, 0:ER])
                        mm.then_inc(t_full, 1)
                    pe.wait_ge(t_done, i * 4 + (2 * k + 2) + 1)
                    pe.wait_ge(w_in[k], i * 32 + 32)
                    for f in range(FC):
                        for half in range(2):
                            j = 2 * f + half
                            if k == 0 and j < 4:
                                pe.wait_ge(h_done, i * (4 * FC) + 1)
                            else:
                                pe.wait_ge(h_done, i * (4 * FC) + (2 * FC * k + j - 3) + 1)
                            pe.matmul(act_bank[j % 4][:, 0:HALF], w1_sb[k][:, f * P:(f + 1) * P],
                                      ebT[k][:].rearrange("p c r -> p (c r)")[:, half * HALF:(half + 1) * HALF],
                                      start=True, stop=True).then_inc(h_full, 1)
                    pe.wait_ge(h_done, i * (4 * FC) + 2 * FC * (k + 1) + 1)
                    for c in range(ET):
                        n = k * ET + c
                        if n < 2:
                            pe.wait_ge(y_done, i * (2 * ET) + 1)
                        else:
                            pe.wait_ge(y_done, i * (2 * ET) + (n - 1) + 1)
                        for f in range(FC):
                            mm = pe.matmul(max_bank[n % 2][0:ER, 0:D], hT[k][:, f, c * ER:(c + 1) * ER],
                                           w2_sb[k][:, f, :], start=(f == 0), stop=(f == FC - 1))
                        mm.then_inc(y_full, 1)

        @block.scalar
        def _(act):
            def move(s, name, lag, dst, last_read, copied=(None, None)):
                if not s.has(lag):
                    act.drain().then_inc(act_done, 1)
                    return
                wait(act, act_full, s.job(ACT_JOBS, name, 0, lag))
                wait(act, *last_read)
                wait(act, *copied)
                nc.scalar.copy(dst[:].rearrange("p a t -> p (a t)"), act_slot(s, name, 0, lag)[:]).then_inc(act_done, 1)

            def step(s):
                for a in range(NA):
                    if not s.has(1):
                        act.drain().then_inc(act_done, 1)
                        continue
                    wait(act, act_full, s.job(ACT_JOBS, "s1", a, 1))
                    if a == 0:
                        wait(act, act_full, s.job(ACT_JOBS, "pv1", 0, 1, 2))
                    nc.scalar.copy(A1[s.slot(1, 2)][:, a].rearrange("p j t -> p (j t)"),
                                   act_slot(s, "s1", a, 1)[:]).then_inc(act_done, 1)
                k = s.slot(1, 2)
                move(s, "kx2", 1, KT2[s.slot(1, 4)], (act_full, s.job(ACT_JOBS, "s2t", NA - 1, 1, 4)),
                     (ke_in[k], s.landed(1, SPREAD, 2, 4)))
                move(s, "qx2", 2, QT2[s.slot(2, 2)], (max_full, s.upto(2, NA, 2)))
                for a in range(NA):
                    if not s.has(3):
                        act.drain().then_inc(act_done, 1)
                        continue
                    wait(act, act_full, s.job(ACT_JOBS, "s2t", a, 3))
                    if a == 0:
                        wait(act, act_full, s.job(ACT_JOBS, "pv2", 0, 3, 2))
                    nc.scalar.activation(P2[s.slot(3, 2)][:, a].rearrange("p j t -> p (j t)"),
                                         act_slot(s, "s2t", a, 3)[:], ACT.Exp, scale=SCALE).then_inc(act_done, 1)
                k = s.slot(0, 2)
                move(s, "qx", 0, QT[k], (qe_in[k], s.landed(0, SPREAD, 2, 2)))
                move(s, "kx", 0, KT[k], (act_full, s.job(ACT_JOBS, "s1", NA - 1, 0, 2)))
                if s.has(4):
                    k = s.slot(4, 2)
                    wait(act, logits_ready, s.upto(4))
                    wait(act, slot_ready, s.upto(4, 1, 2))
                    nc.scalar.activation(lexp[:], lg[k][:], ACT.Exp, bias=nlmax[k][:],
                                         accum_out=esum[k][:]).then_inc(esum_ready, 1)
                if s.has(4):
                    wait(act, x2_ready, s.upto(4), passed)
                    nc.scalar.copy(x2_all[:, bass.ds(s.batch(4), 1), :].rearrange("p o d -> p (o d)"),
                                   x2[s.slot(4, 4)][:]).then_inc(x2_kept, 1)
                if s.has(1):
                    wait(act, x_in[s.slot(1, 4)], s.landed(1, LOADED, 4))
                    wait(act, act_full, s.job(ACT_JOBS, "pv2", 0, 1, 4))
                    nc.scalar.copy(V2[s.slot(1, 4)][:, :, 0:HD],
                                   C[s.slot(1, 4)][:].rearrange("p (h d) -> p h d", d=HD)).then_inc(v2_ready, 1)
                move(s, "pv1", 1, yx1, (dve_full, s.job(DVE_JOBS, "y1", 0, 1, 1)))
                move(s, "pv2", 3, yx2, (dve_full, s.job(DVE_JOBS, "y2", 0, 3, 1)))
                k = s.slot(2, 2)
                move(s, "qm", 2, QM2[k], (qme_in[k], s.landed(2, SPREAD, 2, 2)))

            run(act, step)

            with act.Fori(0, E // 2) as i:
                for k in range(2):
                    for f in range(FC):
                        for half in range(2):
                            j = 2 * f + half
                            wait(act, h_full, i * (4 * FC) + (2 * FC * k + j + 1) + 1, passed)
                            if j == 0:
                                wait(act, y_full, i * (2 * ET) + 1, passed)
                            nc.scalar.activation(hT[k][:, f, half * HALF:(half + 1) * HALF],
                                                 act_bank[j % 4][:, 0:HALF], ACT.Gelu,
                                                 bias=b1T[:, bass.ds(i * (2 * FC) + (k * FC + f), 1)]).then_inc(h_done, 1)

        @block.vector
        def _(dve):
            v = nc.vector
            dve.wait_ge(weights_in, 16 * 9)
            dve.wait_ge(setup_full, 1)
            dve.wait_ge(consts, CONSTS)
            v.tensor_copy(wqkvT[:], max_bank[0][:, 0:3 * D])
            v.tensor_copy(woT[:], max_bank[0][:, 3 * D:4 * D])
            v.tensor_copy(wpT[:], max_bank[1][:, 0:D])
            v.tensor_copy(b1T[:], max_bank[1][:, D:D + E * FC])
            v.tensor_scalar(qkvb[:, 0:2 * D], qkvb[:, 0:2 * D], FEATURE_EPS, None, ALU.add).then_inc(setup_done, 1)
            dve.wait_ge(setup_done, 1)
            for tile in QE + KE2 + QME:
                last = v.memset(tile[:].bitcast(F32), 0.0)
            last.then_inc(spread_zero, 1)
            own = Seq(dve, dve_own, 23, passed)

            def twice(ap):
                return ap.rearrange("p (h d) -> p h d", d=HD).unsqueeze(2).broadcast_to([P, H, 2, HD])

            def moved(s, name, lag, dst):
                if not s.has(lag):
                    dve.drain().then_inc(dve_done, 1)
                    return
                wait(dve, dve_full, s.job(DVE_JOBS, name, 0, lag))
                v.tensor_copy(dst[:], dve_slot(s, name)[:, 0:P]).then_inc(dve_done, 1)

            def normed(s):
                stages = {}
                for name, lag, last_read in (("y1", 1, "y1T"), ("y2", 3, "y2T")):
                    if s.has(lag):
                        wait(dve, dve_full, s.job(DVE_JOBS, name, 0, lag))
                        wait(dve, dve_full, s.job(DVE_JOBS, last_read, 0, lag, 2))
                        yd = stages[name] = dve_slot(s, name)[:].rearrange("p (h d) -> p h d", d=VW)
                        if name == "y1":
                            guarded = own.mark(v.tensor_scalar(den1[:], yd[:, :, HD], DEN_EPS, None, ALU.max))
                        else:
                            inverse2 = own.mark(v.reciprocal(rden2[:], yd[:, :, HD]))
                if "y1" in stages:
                    own.wait(guarded)
                    inverse1 = own.mark(v.reciprocal(rden1[:], den1[:]))
                for name, y, rden in (("y1", y1[s.slot(1, 2)], rden1), ("y2", y2[s.slot(3, 2)], rden2)):
                    if name not in stages:
                        dve.drain().then_inc(dve_done, 1)
                        continue
                    own.wait(inverse1 if name == "y1" else inverse2)
                    v.tensor_tensor(y[:], stages[name][:, :, 0:HD], rden[:].unsqueeze(2).broadcast_to([P, H, HD]),
                                    ALU.mult).then_inc(dve_done, 1)

            def residuals(s):
                parts = [("o1", 1, r1, st1, mv1, ve1, xb[s.slot(1, 2)], xb_ready, var1_ready),
                         ("o2", 3, r2, st2, mv2, ve2, x1b[s.slot(3, 4)], x1b_ready, var2_ready)]
                for name, lag, r, _, _, _, base, ready, _ in parts:
                    if not s.has(lag):
                        dve.drain().then_inc(dve_done, 1)
                        continue
                    wait(dve, dve_full, s.job(DVE_JOBS, name, 0, lag))
                    wait(dve, ready, s.upto(lag))
                    v.tensor_tensor(r[:], dve_slot(s, name)[:, 0:D], base[:], ALU.add).then_inc(dve_done, 1)
                parts = [part for part in parts if s.has(part[1])]
                marks = []
                for name, lag, r, st, *_ in parts:
                    wait(dve, dve_done, s.job(DVE_JOBS, name, 0, lag))
                    marks.append(own.mark(v.bn_stats(st[:], r[:])))
                for k, (_, _, _, st, mv, *_) in enumerate(parts):
                    own.wait(marks[k], alone=True)
                    marks[k] = own.mark(v.bn_aggr(mv[:], st[:]))
                for k, (_, _, _, _, mv, ve, _, _, ready) in enumerate(parts):
                    own.wait(marks[k])
                    v.tensor_scalar(ve[:], mv[:, 1:2], LN_EPS, None, ALU.add).then_inc(ready, 1)

            def step(s):
                moved(s, "xT", 0, xT[s.slot(0, 2)])
                if s.has(2):
                    wait(dve, rstd1_ready, s.upto(2))
                    wait(dve, x1b_ready, s.upto(2, 1, 2))
                    v.tensor_scalar(x1[s.slot(2, 2)][:], r1[:], mv1[:, 0:1], rs1[:], ALU.subtract,
                                    ALU.mult).then_inc(x1_ready, 1)
                    wait(dve, x1_ready, s.upto(2))
                    wait(dve, act_full, s.job(ACT_JOBS, "qm", 0, 2, 2))
                    xx, qx = x1[s.slot(2, 2)][:].rearrange("p (h d) -> p h d", d=HD), QX2[s.slot(2, 2)]
                    own.mark(v.tensor_copy(qx[:, :, 0:2, :], xx.unsqueeze(2).broadcast_to([P, H, 2, HD])))
                    own.wait()
                    v.tensor_tensor(qx[:, :, 2, :], xx, qx[:, :, 0, :].bitcast(F32), ALU.subtract).then_inc(qx2_ready, 1)
                if s.has(4):
                    wait(dve, rstd2_ready, s.upto(4))
                    wait(dve, dve_full, s.job(DVE_JOBS, "x2T", 0, 4, 4))
                    wait(dve, x2_kept, s.upto(4, 1, 4))
                    if s.upto(4, 1, 4) is not None:
                        q = (s.n - 4) // 4
                        wait(dve, scattered[s.slot(4, 4)], 16 * q if s.i is None else s.i * 16 + 16 * q)
                    v.tensor_scalar(x2[s.slot(4, 4)][:], r2[:], mv2[:, 0:1], rs2[:], ALU.subtract,
                                    ALU.mult).then_inc(x2_ready, 1)
                moved(s, "x2T", 4, x2T[s.slot(4, 2)])
                if s.has(0):
                    bank = dve_slot(s, "qkv")
                    wait(dve, dve_full, s.job(DVE_JOBS, "qkv", 0, 0))
                    own.mark(v.tensor_tensor(qkz[:], bank[:, 0:2 * D], qkvb[:, 0:2 * D], ALU.add))
                    wait(dve, act_full, s.job(ACT_JOBS, "pv1", 0, 0, 2))
                    v.tensor_tensor(V1[s.slot(0, 2)][:, :, 0:HD],
                                    bank[:, 2 * D:3 * D].rearrange("p (h d) -> p h d", d=HD),
                                    qkvb[:, 2 * D:3 * D].rearrange("p (h d) -> p h d", d=HD), ALU.add).then_inc(dve_done, 1)
                    own.wait()
                    wait(dve, act_full, s.job(ACT_JOBS, "kx", 0, 0, 2))
                    for stack, high, low, z in ((QX, slice(0, 2), slice(2, 4), qkz[:, 0:D]),
                                                (KX, slice(0, 4, 2), slice(1, 4, 2), qkz[:, D:2 * D])):
                        own.mark(v.tensor_scalar(stack[s.slot(0, 2)][:, :, high, :], twice(z), FEATURE_EPS, None, ALU.max))
                    own.mark(v.tensor_scalar(qk[:], qkz[:], FEATURE_EPS, None, ALU.max))
                    own.wait()
                    for stack, high, low, z in ((QX, slice(0, 2), slice(2, 4), qk[:, 0:D]),
                                                (KX, slice(0, 4, 2), slice(1, 4, 2), qk[:, D:2 * D])):
                        last = v.tensor_tensor(stack[s.slot(0, 2)][:, :, low, :], twice(z),
                                               stack[s.slot(0, 2)][:, :, high, :].bitcast(F32), ALU.subtract)
                    last.then_inc(qkx_ready, 1)
                else:
                    dve.drain().then_inc(dve_done, 1)
                if s.has(4):
                    k = s.slot(4, 2)
                    wait(dve, dve_full, s.job(DVE_JOBS, "lg", 0, 4))
                    wait(dve, esum_ready, s.upto(4, 1, 2))
                    v.tensor_copy(lg[k][:], dve_slot(s, "lg")[:, 0:E]).then_inc(dve_done, 1)
                    wait(dve, dve_done, s.job(DVE_JOBS, "lg", 0, 4))
                    own.mark(v.tensor_reduce(lmax[:], lg[k][:], AX_X, ALU.max))
                    own.wait()
                    v.tensor_scalar(nlmax[k][:], lmax[:], -1.0, None, ALU.mult).then_inc(logits_ready, 1)
                    own.mark(v.scalar_tensor_tensor(out=cand[:], in0=lg[k][:], scalar=lmax[:], in1=rank_w[:],
                                                    op0=ALU.is_ge, op1=ALU.mult))
                    own.wait()
                    own.mark(v.tensor_reduce(top[k][:], cand[:], AX_X, ALU.max))
                    own.wait()
                    wait(dve, dve_full, s.job(DVE_JOBS, "rk", 0, 4, 2))
                    v.tensor_scalar(oh[k][:], cand[:], top[k][:], None, ALU.is_equal).then_inc(oh_ready, 1)
                else:
                    dve.drain().then_inc(dve_done, 1)
                if s.has(2):
                    wait(dve, qm_ready, s.upto(2, 1, 2))
                    for a in range(NA):
                        wait(dve, max_full, s.upto(2, NA, 0, a + 1 - NA))
                        v.tensor_reduce(mx[s.slot(2, 2)][:, a * G:(a + 1) * G],
                                        max_bank[a % 2][:].rearrange("p (j t) -> p j t", j=G),
                                        AX_X, ALU.max).then_inc(max_done, 1)
                if s.has(4):
                    k, b = s.slot(4, 2), s.batch(4)
                    bank = dve_slot(s, "rk")
                    wait(dve, dve_full, s.job(DVE_JOBS, "rk", 0, 4))
                    wait(dve, oh_ready, s.upto(4))
                    own.mark(v.tensor_tensor(rc[:], bank[:, 0:E], carry[k][:], ALU.add))
                    v.tensor_tensor(carry[1 - k][:], bank[:, E:2 * E], carry[k][:], ALU.add).then_inc(dve_done, 1)
                    own.wait()
                    own.mark(v.tensor_tensor_reduce(rcoh[:], rc[:], oh[k][:], 1.0, 0.0, ALU.mult, ALU.add, rank[:]))
                    own.mark(v.tensor_scalar(slot0[:], top[k][:], -float(CAPP), float(E * CAPP - 1), ALU.mult, ALU.add))
                    own.wait()
                    own.mark(v.tensor_scalar(over[:], rank[:], float(CAP), BIG, ALU.is_gt, ALU.mult))
                    own.mark(v.tensor_tensor(slot1[:], slot0[:], rank[:], ALU.add))
                    own.mark(v.tensor_scalar(valid[:], rank[:], float(CAP), None, ALU.is_le))
                    wait(dve, esum_ready, s.upto(4))
                    own.mark(v.reciprocal(rsum[:], esum[k][:]))
                    own.wait()
                    own.mark(v.tensor_tensor(slot2[:], slot1[:], over[:], ALU.add))
                    v.tensor_tensor(gate_all[:, bass.ds(b, 1)], rsum[:], valid[:], ALU.mult)
                    own.wait()
                    if s.upto(4, 1, 4) is not None:
                        q = (s.n - 4) // 4
                        wait(dve, scattered[s.slot(4, 4)], 16 * q if s.i is None else s.i * 16 + 16 * q)
                    v.tensor_scalar(gidx_all[:, bass.ds(b, 1)], slot2[:], float(TRASH), None, ALU.min)
                    v.tensor_copy(sidx[s.slot(4, 4)][:], slot2[:]).then_inc(slot_ready, 1)
                else:
                    dve.drain().then_inc(dve_done, 1)
                normed(s)
                moved(s, "y1T", 1, y1T[s.slot(1, 2)])
                moved(s, "y2T", 3, y2T[s.slot(3, 2)])
                residuals(s)

            run_own(dve, own, step)

            with dve.Fori(0, E // 2) as i:
                for k in range(2):
                    for n, (c0, c1) in enumerate([(0, 4), (4, ET)]):
                        dve.wait_ge(t_full, i * 4 + (2 * k + n + 1))
                        if n == 0:
                            dve.wait_ge(h_full, i * (4 * FC) + 1)
                        v.tensor_copy(ebT[k][:, c0:c1, :].rearrange("p c r -> p (c r)"),
                                      dve_bank[n][:, 0:(c1 - c0) * ER]).then_inc(t_done, 1)
                    for c in range(ET):
                        n = k * ET + c
                        dve.wait_ge(y_full, i * (2 * ET) + (n + 1) + 1)
                        if c == 0:
                            dve.wait_ge(ye_out[k], i * 16 + 16)
                        v.tensor_tensor(yE[k][:, c, :], max_bank[n % 2][0:ER, 0:D],
                                        b2b[0:ER, bass.ds(i * 2 + k, 1), :].rearrange("p o d -> p (o d)"),
                                        ALU.add).then_inc(y_done, 1)

            with dve.Fori(0, B // GR // 2) as i:
                for k in range(2):
                    dve.wait_ge(gathered[k], i * (16 * GR) + 16 * GR)
                    dve.wait_ge(x2_kept, B)
                    for c in range(GR):
                        b = i * (2 * GR) + (k * GR + c)
                        v.scalar_tensor_tensor(out=r3[k][:, c, :], in0=gy[k][:, c, :], scalar=gate_all[:, bass.ds(b, 1)],
                                               in1=x2_all[:, bass.ds(b, 1), :].rearrange("p o d -> p (o d)"),
                                               op0=ALU.mult, op1=ALU.add).then_inc(comb_own, 1)
                    for c in range(GR):
                        dve.wait_ge(comb_own, i * (2 * COMB) + (k * COMB + c + 1))
                        v.bn_stats(st3[:, c, :], r3[k][:, c, :]).then_inc(comb_own, 1)
                    for c in range(GR):
                        wait(dve, comb_own, i * (2 * COMB) + (k * COMB + GR + c + 1), passed)
                        v.bn_aggr(mv3[k][:, c, :], st3[:, c, :]).then_inc(comb_own, 1)
                    dve.wait_ge(comb_own, i * (2 * COMB) + (k + 1) * COMB)
                    v.tensor_scalar(ve3[k][:], mv3[k][:, :, 1], LN_EPS, None, ALU.add).then_inc(var3_ready, 1)
                    dve.wait_ge(rstd3_ready, i * 2 + (k + 1))
                    dve.wait_ge(out_done[k], i * 16 + 16)
                    for c in range(GR):
                        v.tensor_scalar(ot[k][:, c, :], r3[k][:, c, :], mv3[k][:, c, 0:1], rs3[k][:, c:c + 1],
                                        ALU.subtract, ALU.mult).then_inc(ot_ready, 1)


_INS = ['x', 'ctx_1024', 'L0_attn_qkv_w', 'L0_attn_qkv_b', 'L0_attn_out_w', 'L0_attn_out_b',
        'L0_xattn_W_proj', 'L0_xattn_b_proj', 'L0_ffn_wg', 'L0_ffn_W1', 'L0_ffn_b1', 'L0_ffn_W2', 'L0_ffn_b2']


def kernel(**inputs):
    import numpy as _np
    import concourse.bacc as _bacc
    from concourse import mybir as _mybir
    from concourse.bass_utils import run_bass_kernel_spmd as _run

    nc = _bacc.Bacc("TRN2", target_bir_lowering=False, num_devices=1)
    arrays, args = {}, []
    for name in _INS:
        a = _np.ascontiguousarray(inputs[name])
        arrays[f"in_{name}"] = a
        args.append(nc.dram_tensor(f"in_{name}", a.shape, _mybir.dt.from_np(a.dtype), kind="ExternalInput").ap())
    shape = tuple(inputs['x'].shape)
    args.append(nc.dram_tensor("out_x", shape, _mybir.dt.from_np(_np.dtype('float32')), kind="ExternalOutput").ap())
    decoder(nc, *args)
    r = _run(nc, [arrays], core_ids=[0])
    return r.results[0]["out_x"]
```
